# Optimizing a Trainium2 kernel written in Bass

```python
import numpy as np
import jax
import jax.numpy as jnp

def _softmax(x, axis=-1):
    return jax.nn.softmax(x, axis=axis)

def _gelu(x):
    return jax.nn.gelu(x, approximate=True)

def _silu(x):
    return jax.nn.silu(x)

def _sigmoid(x):
    return jax.nn.sigmoid(x)

def _layernorm(x, axis=-1, eps=1e-05):
    m = jnp.mean(x, axis=axis, keepdims=True)
    v = jnp.var(x, axis=axis, keepdims=True)
    return (x - m) / jnp.sqrt(v + eps)

def _scatter_add(tgt, idx, src, axis=0):
    return tgt.at[idx].add(src)

def _segment_sum(src, seg, n):
    return jax.ops.segment_sum(src, seg, n)
kernel_name = 'mk_prb_d1_jaxref_r8_487780'

def setup_inputs(seed: int=0):
    np.random.seed(seed)
    _w = jnp.asarray

    def _L0_attn_setup():
        import jax, jax.numpy as jnp
        import numpy as np
        B, S, H = (2, 1024, 128)
        NUM_HEADS = 16
        HEAD_DIM = H // NUM_HEADS
        KERNEL = 7
        DILATION = 1
        SCALE = 1.0 / np.sqrt(HEAD_DIM)
        key = jax.random.key(seed)
        ks = jax.random.split(key, 9)
        init = 0.02
        return {'hidden_states': jax.random.normal(ks[0], (B, S, H), dtype=jnp.float32), 'w_q': jax.random.normal(ks[1], (H, H), dtype=jnp.float32) * init, 'b_q': jnp.zeros((H,), dtype=jnp.float32), 'w_k': jax.random.normal(ks[2], (H, H), dtype=jnp.float32) * init, 'b_k': jnp.zeros((H,), dtype=jnp.float32), 'w_v': jax.random.normal(ks[3], (H, H), dtype=jnp.float32) * init, 'b_v': jnp.zeros((H,), dtype=jnp.float32), 'w_o': jax.random.normal(ks[4], (H, H), dtype=jnp.float32) * init, 'b_o': jnp.zeros((H,), dtype=jnp.float32)}
    _L0_attn_in = _L0_attn_setup()

    def _L0_ffn_setup():
        import jax, jax.numpy as jnp
        import numpy as np
        E = 8
        K = 2
        R = 64
        ALPHA = 128.0
        SCALING = ALPHA / R
        key = jax.random.key(seed)
        k0, k1, k2, k3 = jax.random.split(key, 4)
        B, S, D = (4, 512, 128)
        x = jax.random.normal(k0, (B, S, D), jnp.float32)
        Wg = jax.random.normal(k1, (E, D), jnp.float32) * 0.02
        bg = jnp.zeros((E,), jnp.float32)
        W1 = jax.random.normal(k2, (E, R, D), jnp.float32) * (1.0 / np.sqrt(D))
        W2 = jax.random.normal(k3, (E, D, R), jnp.float32) * 0.02
        return {'x': x, 'Wg': Wg, 'bg': bg, 'W1': W1, 'W2': W2}
    _L0_ffn_in = _L0_ffn_setup()
    _d = {'L0_attn_hidden_states': _L0_attn_in['hidden_states'], 'L0_attn_w_q': _L0_attn_in['w_q'], 'L0_attn_b_q': _L0_attn_in['b_q'], 'L0_attn_w_k': _L0_attn_in['w_k'], 'L0_attn_b_k': _L0_attn_in['b_k'], 'L0_attn_w_v': _L0_attn_in['w_v'], 'L0_attn_b_v': _L0_attn_in['b_v'], 'L0_attn_w_o': _L0_attn_in['w_o'], 'L0_attn_b_o': _L0_attn_in['b_o'], 'L0_ffn_Wg': _L0_ffn_in['Wg'], 'L0_ffn_bg': _L0_ffn_in['bg'], 'L0_ffn_W1': _L0_ffn_in['W1'], 'L0_ffn_W2': _L0_ffn_in['W2']}
    _x0 = _d['L0_attn_hidden_states']
    _d['L0_attn_hidden_states'] = jax.random.normal(jax.random.fold_in(jax.random.key(seed), 1), (16, 512, 128), dtype=_x0.dtype)
    del _x0
    return _d

def reference(L0_attn_hidden_states, L0_attn_w_q, L0_attn_b_q, L0_attn_w_k, L0_attn_b_k, L0_attn_w_v, L0_attn_b_v, L0_attn_w_o, L0_attn_b_o, L0_ffn_Wg, L0_ffn_bg, L0_ffn_W1, L0_ffn_W2):

    def _L0_attn_ref(hidden_states, w_q, b_q, w_k, b_k, w_v, b_v, w_o, b_o):
        import jax, jax.numpy as jnp
        import numpy as np
        B, S, H = (2, 1024, 128)
        NUM_HEADS = 16
        HEAD_DIM = H // NUM_HEADS
        KERNEL = 7
        DILATION = 1
        SCALE = 1.0 / np.sqrt(HEAD_DIM)
        b, s, h = hidden_states.shape
        q = hidden_states @ w_q + b_q
        k = hidden_states @ w_k + b_k
        v = hidden_states @ w_v + b_v
        q = q.reshape(b, s, NUM_HEADS, HEAD_DIM).transpose(0, 2, 1, 3)
        k = k.reshape(b, s, NUM_HEADS, HEAD_DIM).transpose(0, 2, 1, 3)
        v = v.reshape(b, s, NUM_HEADS, HEAD_DIM).transpose(0, 2, 1, 3)
        offsets = (jnp.arange(KERNEL) - KERNEL // 2) * DILATION
        idx = jnp.arange(s)[:, None] + offsets[None, :]
        valid = (idx >= 0) & (idx < s)
        idx_c = jnp.clip(idx, 0, s - 1)
        k_win = k[:, :, idx_c, :]
        v_win = v[:, :, idx_c, :]
        scores = jnp.einsum('bhsd,bhskd->bhsk', q, k_win) * SCALE
        scores = jnp.where(valid[None, None], scores, -jnp.inf)
        attn = jax.nn.softmax(scores, axis=-1)
        out = jnp.einsum('bhsk,bhskd->bhsd', attn, v_win)
        out = out.transpose(0, 2, 1, 3).reshape(b, s, h)
        return out @ w_o + b_o

    def _L0_ffn_ref(x, Wg, bg, W1, W2):
        import jax, jax.numpy as jnp
        import numpy as np
        E = 8
        K = 2
        R = 64
        ALPHA = 128.0
        SCALING = ALPHA / R
        orig_shape = x.shape
        D = orig_shape[-1]
        xf = x.reshape(-1, D)
        logits = xf @ Wg.T + bg
        top_gates, top_idx = jax.lax.top_k(logits, K)
        top_gates = jax.nn.softmax(top_gates, axis=-1)
        h = jax.nn.gelu(jnp.einsum('nd,erd->enr', xf, W1), approximate=False)
        eout = SCALING * jnp.einsum('enr,edr->ned', h, W2)
        sel = jnp.take_along_axis(eout, top_idx[:, :, None], axis=1)
        out = jnp.sum(top_gates[:, :, None] * sel, axis=1)
        return out.reshape(orig_shape)
    x = L0_attn_hidden_states
    xn = _layernorm(x, axis=-1)
    x = x + _L0_attn_ref(xn, L0_attn_w_q, L0_attn_b_q, L0_attn_w_k, L0_attn_b_k, L0_attn_w_v, L0_attn_b_v, L0_attn_w_o, L0_attn_b_o) + _L0_ffn_ref(xn, L0_ffn_Wg, L0_ffn_bg, L0_ffn_W1, L0_ffn_W2)
    return x

_drawn_inputs = setup_inputs


def setup_inputs(seed=0):
    import zlib

    import numpy as np

    out = dict(_drawn_inputs(seed))
    spreads = {'L0_attn_b_q': (0.0, 0.8),
     'L0_attn_b_k': (0.0, 0.8),
     'L0_attn_b_v': (0.0, 0.333),
     'L0_attn_b_o': (0.0, 0.1),
     'L0_ffn_bg': (0.0, 0.1)}
    factors = {'L0_attn_w_q': 8.0, 'L0_attn_w_k': 8.0, 'L0_attn_w_v': 2.969}
    for name, (base, spread) in spreads.items():
        noise = np.random.default_rng([zlib.crc32(name.encode()), seed]).standard_normal(out[name].shape)
        drawn = base * np.exp(spread * noise) if base else spread * noise
        out[name] = jnp.asarray(drawn.astype(out[name].dtype))
    for name, factor in factors.items():
        out[name] = (out[name] * factor).astype(out[name].dtype)
    return out
```

```python
import numpy as np
import concourse.bass as bass
from concourse import mybir
from contextlib import ExitStack

BATCH, SEQ, DIM = 16, 512, 128
HEADS, HEAD_DIM = 16, 8
WINDOW, REACH = 7, 3
EXPERTS, RANK = 8, 64
SCALING = 128.0 / RANK
SCALE = HEAD_DIM ** -0.5
EPS = 1e-5
P = 128

TOKENS = BATCH * SEQ
PER = TOKENS // P
PARTS = SEQ // PER
HALO = 2 * REACH
SLOTS = PER + HALO
GROUP = 8
GROUPS = PER // GROUP
HALF = GROUP // 2
K0 = 2 * GROUP
V0 = K0 + SLOTS
HD = HALF * DIM
WH = WINDOW * HEADS
HW = HALF * HEADS
CHUNKS = EXPERTS * RANK // P
PER_CHUNK = P // RANK
GW = GROUP * EXPERTS

C_IDENT = 0
C_TIE = C_IDENT + P
C_EDGE = C_TIE + GW
C_NORM = C_EDGE + 2
NORM_CONSTANTS = (0.5, DIM / 4, 1 / DIM, EPS, -0.5)
C_KEEP = C_NORM + GROUP * len(NORM_CONSTANTS)
C_SEL = C_KEEP
C_ONES = C_SEL + CHUNKS * P
C_ALL = C_ONES + P
NORM_STEPS = 11
NEVER = -1e30
TAKEN = -3e38

FRONT_HALO = 2 + HALO
FRONT = 2 + GROUP + 2 * CHUNKS


def front_base(n):
    return 0 if isinstance(n, int) and n < 0 else FRONT_HALO + n * FRONT


def constants():
    c = np.zeros((P, C_ALL), np.float32)
    c[:, C_IDENT:C_IDENT + P] = np.eye(P)
    c[:, C_TIE:C_TIE + GW] = np.tile(np.arange(EXPERTS, 0, -1), GROUP)
    for m in range(CHUNKS):
        for r in range(P):
            for part in range(2):
                c[EXPERTS * part + m * PER_CHUNK + r // RANK, C_SEL + m * P + r] = SCALING
    c[0, C_ONES:C_ONES + P] = 1.0
    c[32, C_ONES:C_ONES + P] = 1.0
    c[0::PARTS, C_EDGE] = NEVER
    c[PARTS - 1::PARTS, C_EDGE + 1] = NEVER
    for i, value in enumerate(NORM_CONSTANTS):
        c[:, C_NORM + i * GROUP:C_NORM + (i + 1) * GROUP] = value
    return c


def attention_and_experts(nc, x, wq, bq, wk, bk, wv, bv, wo, bo, wg, bg, w1, w2, const, out):
    f32, f32r = mybir.dt.float32, mybir.dt.float32r
    ALU, ACT, AX = mybir.AluOpType, mybir.ActivationFunctionType, mybir.AxisListType.X
    x_tok = x.rearrange("b s h -> (b s) h")
    x_view = x_tok.rearrange("(p j) h -> p j h", j=PER)
    out_view = out.rearrange("b s h -> (b s) h").rearrange("(p j) h -> p j h", j=PER)

    with ExitStack() as ctx:
        def sb(name, shape, dt=f32):
            return ctx.enter_context(nc.sbuf_tensor(name, shape, dt))

        def pb(name):
            return ctx.enter_context(nc.psum_tensor(name, [P, 512], f32))

        def sem(name):
            return ctx.enter_context(nc.semaphore(name))

        X = sb("X", [P, PER, DIM])
        KV = sb("KV", [P, V0 + SLOTS, DIM])
        const_sb = sb("const_sb", [P, C_KEEP])
        w_qkv = sb("w_qkv", [P, 3, DIM])
        w_out = sb("w_out", [P, DIM])
        w_gate = sb("w_gate", [P, EXPERTS])
        w1_sb = sb("w1_sb", [P, CHUNKS * P])
        w2_sb = sb("w2_sb", [P, CHUNKS, DIM])
        b_out = sb("b_out", [P, DIM])
        bias_r = sb("bias_r", [64, 3 * DIM + GW], f32r)
        ones_r = sb("ones_r", [64, P], f32r)
        sel_r = sb("sel_r", [64, CHUNKS * P], f32r)
        st6 = sb("st6", [P, GROUP, 6])
        mean = sb("mean", [P, GROUP])
        dif = sb("dif", [P, GROUP])
        rstd = sb("rstd", [P, GROUP])
        xn = sb("xn", [P, GROUP, DIM])
        xnT = sb("xnT", [P, GROUP, P])
        prod = [sb(f"prod{h}", [P, WINDOW, HD]) for h in range(2)]
        XH = bass.AP(prod[0][:].tensor, 0, [list(prod[0][:].ap[0]), [DIM, HALO], [1, DIM]])
        const_raw = bass.AP(prod[1][:].tensor, 2 * HD, [[prod[1][:].ap[0][0], 64], [1, C_ALL - C_KEEP]])
        bias_raw = prod[1][0:64, 0, 0:3 * DIM + GW]
        bias_hi = prod[1][0:64, 1, 0:3 * DIM + GW].bitcast(f32r)
        scT = [sb(f"scT{h}", [P, HD]) for h in range(2)]
        sc = [sb(f"sc{h}", [P, WINDOW, HW]) for h in range(2)]
        smax = [sb(f"smax{h}", [P, HW]) for h in range(2)]
        ssum = [sb(f"ssum{h}", [P, HW]) for h in range(2)]
        srec = [sb(f"srec{h}", [P, HW]) for h in range(2)]
        oT_sb = scT
        hid = sb("hid", [P, 2, CHUNKS, HD])
        hidg = sb("hidg", [P, 2, CHUNKS, HD])
        g_top = sb("g_top", [P, 4, GROUP])
        g_dif = sb("g_dif", [P, GW])
        g_tmp = sb("g_tmp", [P, GW])
        g_sel1 = sb("g_sel1", [P, GW])
        g_sel2 = sb("g_sel2", [P, GW])
        g_exp = sb("g_exp", [P, GW])
        g_sum = sb("g_sum", [P, GROUP])
        g_rec = sb("g_rec", [P, GROUP])
        gates = sb("gates", [P, GROUP, 2 * EXPERTS], f32r)
        gT = sb("gT", [64, GROUP * P], f32r)

        front = [pb("front0"), pb("front1")]
        gbank = [pb("gbank0"), pb("gbank1")]
        chain = [pb("chain0"), pb("chain1")]
        ybank = [pb("ybank0"), pb("ybank1")]

        ident = const_sb[:, C_IDENT:C_IDENT + P]
        tie = const_sb[:, C_TIE:C_TIE + GW]
        edge = [const_sb[:, C_EDGE:C_EDGE + 1], const_sb[:, C_EDGE + 1:C_EDGE + 2]]
        half, quarter_dim, per_dim, eps, minus_half = (
            const_sb[:, C_NORM + i * GROUP:C_NORM + (i + 1) * GROUP] for i in range(len(NORM_CONSTANTS)))

        s_const = sem("s_const")
        s_wproj = sem("s_wproj")
        s_wffn = sem("s_wffn")
        s_halo0 = sem("s_halo0")
        s_halo = sem("s_halo")
        s_x = sem("s_x")
        s_prep = sem("s_prep")
        s_zero = sem("s_zero")
        s_stat = sem("s_stat")
        s_rstd = sem("s_rstd")
        s_xn = sem("s_xn")
        s_xb = sem("s_xb")
        s_front = sem("s_front")
        s_front_free = sem("s_front_free")
        s_logit = sem("s_logit")
        s_top = sem("s_top")
        s_gexp = sem("s_gexp")
        s_gate = sem("s_gate")
        s_gT = sem("s_gT")
        s_gT_sb = sem("s_gT_sb")
        s_gb = sem("s_gb")
        s_hid = sem("s_hid")
        s_hidg = sem("s_hidg")
        s_qk = sem("s_qk")
        s_scT = sem("s_scT")
        s_scT_sb = sem("s_scT_sb")
        s_score = sem("s_score")
        s_mask = sem("s_mask")
        s_max = sem("s_max")
        s_dif = sem("s_dif")
        s_exp = sem("s_exp")
        s_sum = sem("s_sum")
        s_rec = sem("s_rec")
        s_prob = sem("s_prob")
        s_pv = sem("s_pv")
        s_oT = sem("s_oT")
        s_oT_sb = sem("s_oT_sb")
        s_w2 = sem("s_w2")
        s_y = sem("s_y")
        s_res = sem("s_res")
        s_store = sem("s_store")

        def windows(place, first):
            a = KV[:, bass.ds(first + place, HALF), :]
            return bass.AP(a.tensor, a.offset, [list(a.ap[0]), [DIM, WINDOW], [1, HD]])

        def spread(a, *dims):
            return bass.AP(a.tensor, a.offset, [list(a.ap[0]), *map(list, dims)])


        block = ctx.enter_context(nc.Block())

        @block.sync
        def _(sp):
            sp.dma_start(const_sb[:], const[:, 0:C_KEEP]).then_inc(s_const, 16)
            sp.dma_start(const_raw, const[0:64, C_KEEP:C_ALL]).then_inc(s_const, 16)
            sp.wait_ge(s_halo0, 1)
            for a, b in ((1, 16), (16, P)):
                src = x_tok[a * PER - REACH:b * PER - REACH, :].rearrange("(p j) h -> p j h", j=PER)
                sp.dma_start(XH[a:b, 0:REACH, :], src[:, 0:REACH, :]).then_inc(s_halo, 16)
            for a, b in ((0, P - 16), (P - 16, P - 1)):
                src = x_tok[(a + 1) * PER:(b + 1) * PER, :].rearrange("(p j) h -> p j h", j=PER)
                sp.dma_start(XH[a:b, REACH:HALO, :], src[:, 0:REACH, :]).then_inc(s_halo, 16)
            sp.dma_start(X[:, 0:GROUP, :], x_view[:, 0:GROUP, :]).then_inc(s_x, 16)
            with sp.Fori(1, GROUPS) as n:
                sp.wait_ge(s_x, 16 * n)
                sp.dma_start(X[:, bass.ds(n * GROUP, GROUP), :],
                             x_view[:, bass.ds(n * GROUP, GROUP), :]).then_inc(s_x, 16)
            with sp.Fori(0, GROUPS) as n:
                sp.wait_ge(s_res, 2 * n + 2)
                sp.dma_start(out_view[:, bass.ds(n * GROUP, GROUP), :],
                             X[:, bass.ds(n * GROUP, GROUP), :]).then_inc(s_store, 16)
            sp.wait_ge(s_store, 16 * GROUPS)

        @block.gpsimd
        def _(pool):
            nc.gpsimd.memset(XH[:], 0.0).then_inc(s_halo0, 1)
            pool.wait_ge(s_const, 16 * 11)

            def normalise(stage, src, count):
                step = [0]

                def op(out, in0, in1, alu):
                    step[0] += 1
                    nc.gpsimd.tensor_tensor(out, in0, in1, alu).then_inc(s_rstd, 1)

                def wait():
                    pool.wait_ge(s_rstd, NORM_STEPS * stage + step[0])

                def col(a):
                    return a[:, 0:count]

                pool.wait_ge(s_stat, stage + 1)
                op(col(mean), st6[:, 0:count, 1], st6[:, 0:count, 4], ALU.add)
                op(col(dif), st6[:, 0:count, 1], st6[:, 0:count, 4], ALU.subtract)
                op(col(rstd), st6[:, 0:count, 2], st6[:, 0:count, 5], ALU.add)
                wait()
                op(col(mean), col(mean), col(half), ALU.mult)
                op(col(dif), col(dif), col(dif), ALU.mult)
                wait()
                op(col(dif), col(dif), col(quarter_dim), ALU.mult)
                wait()
                op(col(rstd), col(rstd), col(dif), ALU.add)
                wait()
                op(col(rstd), col(rstd), col(per_dim), ALU.mult)
                wait()
                op(col(rstd), col(rstd), col(eps), ALU.add)
                wait()
                op(col(rstd), col(rstd), col(minus_half), ALU.pow)
                if not isinstance(stage, int) or stage >= 1:
                    pool.wait_ge(s_front, front_base(stage - 2) + 2)
                op(xn[:, 0:count, :], src, spread(mean[:, 0:1], [1, count], [0, DIM]), ALU.subtract)
                wait()
                nc.gpsimd.tensor_tensor(xn[:, 0:count, :], xn[:, 0:count, :],
                                        spread(rstd[:, 0:1], [1, count], [0, DIM]),
                                        ALU.mult).then_inc(s_xn, 1)
                assert step[0] == NORM_STEPS

            def group_in(n):
                normalise(n + 1, X[:, bass.ds(n * GROUP, GROUP), :], GROUP)

            def add_bias(n):
                xs = X[:, bass.ds(n * GROUP, GROUP), :]
                nc.gpsimd.tensor_tensor(xs, xs, spread(b_out[:, 0:1], [0, GROUP], [1, DIM]),
                                        ALU.add).then_inc(s_xb, 1)

            def probabilities(t, h):
                pool.wait_ge(s_rec, 2 * t + h + 1)
                if not isinstance(t, int) or t >= 1:
                    pool.wait_ge(s_pv, 2 * t + h - 1)
                nc.gpsimd.tensor_tensor(sc[h][:], sc[h][:],
                                        spread(srec[h][:, 0:1], [0, WINDOW], [1, HW]),
                                        ALU.mult).then_inc(s_prob, 1)

            def body(t, attend, ahead):
                if ahead:
                    group_in(t + 2)
                if attend:
                    for h in range(2):
                        probabilities(t, h)
                if ahead:
                    add_bias(t + 2)

            normalise(0, XH[:], HALO)
            group_in(0)
            add_bias(0)
            body(-1, False, True)
            body(0, True, True)
            with pool.Fori(1, GROUPS - 2) as t:
                body(t, True, True)
            body(GROUPS - 2, True, False)
            body(GROUPS - 1, True, False)

        @block.scalar
        def _(act):
            act.dma_start(b_out[:], bo.rearrange("(a n) -> a n", a=1).broadcast_to([P, DIM])).then_inc(s_const, 16)
            act.wait_ge(s_zero, 3)
            for row in (0, 32):
                for i, b in enumerate((bq, bk, bv)):
                    act.dma_start(bias_raw[row:row + 1, i * DIM:(i + 1) * DIM],
                                  b.rearrange("(a n) -> a n", a=1)).then_inc(s_const, 16)
                act.dma_start(bias_raw[row:row + 1, 3 * DIM:].rearrange("a (g e) -> a g e", g=GROUP),
                              bass.AP(bg.tensor, bg.offset, [[0, 1], [0, GROUP], [1, EXPERTS]]))\
                    .then_inc(s_const, 16)
            for i, w in enumerate((wq, wk, wv)):
                act.dma_start(w_qkv[:, i, :], w).then_inc(s_wproj, 16)
            act.dma_start(w_gate[:], wg).then_inc(s_wproj, 16)
            act.dma_start(w1_sb[:], w1).then_inc(s_wffn, 16)
            act.dma_start(w2_sb[:], w2.rearrange("(c p) n -> p c n", p=P)).then_inc(s_wffn, 16)
            act.dma_start(w_out[:], wo).then_inc(s_wffn, 16)

            def rows_in(n, counts):
                for h, count in enumerate(counts):
                    act.wait_ge(s_front, front_base(n) + h + 1)
                    act.activation(xnT[:, h * HALF:h * HALF + count, :],
                                   front[h][:, 0:count * P], ACT.Copy).then_inc(s_front_free, 1)

            def project(n, slots):
                for j, slot in enumerate(slots):
                    act.wait_ge(s_front, front_base(n) + 2 + j + 1)
                    if not isinstance(n, int) or n >= 0:
                        if j == 0 and (not isinstance(n, int) or n >= 2):
                            act.wait_ge(s_qk, 2 * n - 2)
                        act.activation(KV[:, bass.ds(n * GROUP + j, 1), :],
                                       front[j % 2][:, 0:DIM], ACT.Copy)
                    a = KV[:, bass.ds(slot + K0, 1), :]
                    act.activation(bass.AP(a.tensor, a.offset, [list(a.ap[0]), [SLOTS * DIM, 2], [1, DIM]]),
                                   front[j % 2][:, DIM:3 * DIM].rearrange("p (c n) -> p c n", c=2),
                                   ACT.Copy).then_inc(s_front_free, 1)

            def hidden(n, h):
                for m in range(CHUNKS):
                    i = h * CHUNKS + m
                    act.wait_ge(s_front, front_base(n) + 2 + GROUP + i + 1)
                    if not isinstance(n, int) or n >= 1:
                        act.wait_ge(s_hidg, 2 * CHUNKS * (n - 1) + i + 1)
                    act.activation(hid[:, h, m, :], front[i % 2][:], ACT.Gelu)\
                        .then_inc(s_front_free, 1)

            def gates_in(n):
                for h in range(2):
                    act.wait_ge(s_gT, 2 * n + h + 1)
                    act.activation(gT[0:2 * EXPERTS, h * HD:(h + 1) * HD],
                                   gbank[h][0:2 * EXPERTS, :], ACT.Copy)\
                        .then_inc(s_gT_sb, 1)

            def body(t, attend, after):
                u = t + 1
                if after:
                    rows_in(u, (HALF, HALF))
                    project(u, [u * GROUP + REACH + j for j in range(GROUP)])
                if attend:
                    for h in range(2):
                        act.wait_ge(s_scT, 2 * t + h + 1)
                        act.activation(scT[h][0:WH, :], chain[h][0:WH, :], ACT.Copy).then_inc(s_scT_sb, 1)
                if after:
                    act.wait_ge(s_top, TOP_STEPS * u + 2)
                    if not isinstance(u, int) or u >= 1:
                        act.wait_ge(s_gate, u)
                    act.activation(g_exp[:], g_dif[:], ACT.Exp).then_inc(s_gexp, 1)
                if attend:
                    for h in range(2):
                        act.wait_ge(s_dif, 2 * t + h + 1)
                        act.activation(sc[h][:], sc[h][:], ACT.Exp, scale=SCALE).then_inc(s_exp, 1)
                if after:
                    hidden(u, 0)
                    gates_in(u)
                    hidden(u, 1)
                if attend:
                    for h in range(2):
                        act.wait_ge(s_oT, 2 * t + h + 1)
                        act.activation(oT_sb[h][:], chain[h][:], ACT.Copy).then_inc(s_oT_sb, 1)

            rows_in(-1, (HALF, HALO - HALF))
            project(-1, [j if j < REACH else PER + j for j in range(HALO)])
            body(-1, False, True)
            with act.Fori(0, GROUPS - 1) as t:
                body(t, True, True)
            body(GROUPS - 1, True, False)

        @block.vector
        def _(dve):
            nc.vector.memset(bias_raw[:], 0.0).then_inc(s_zero, 1)
            nc.vector.memset(bias_r[:].bitcast(f32), 0.0).then_inc(s_zero, 1)
            nc.vector.memset(gT[:].bitcast(f32), 0.0).then_inc(s_zero, 1)
            dve.wait_ge(s_zero, 3)
            dve.wait_ge(s_const, 16 * 11)
            nc.vector.tensor_copy(ones_r[:], const_raw[:, C_ONES - C_KEEP:C_ONES - C_KEEP + P]).then_inc(s_prep, 1)
            nc.vector.tensor_copy(sel_r[:], const_raw[:, 0:CHUNKS * P]).then_inc(s_prep, 1)
            nc.vector.tensor_copy(bias_hi[:], bias_raw[:]).then_inc(s_prep, 1)
            dve.wait_ge(s_prep, 3)
            nc.vector.tensor_copy(bias_r[0:32, :], bias_hi[0:32, :].bitcast(f32)).then_inc(s_prep, 1)
            nc.vector.tensor_tensor(bias_r[32:64, :], bias_raw[32:64, :],
                                    bias_hi[32:64, :].bitcast(f32), ALU.subtract).then_inc(s_prep, 1)

            def statistics(stage, row, count):
                if not isinstance(stage, int) or stage >= 1:
                    dve.wait_ge(s_xn, stage)
                for j in range(count):
                    last = nc.vector.bn_stats(st6[:, j, :], row(j))
                last.then_inc(s_stat, 1)

            def group_statistics(n):
                dve.wait_ge(s_x, 16 * (n + 1))
                statistics(n + 1, lambda j: X[:, bass.ds(n * GROUP + j, 1), :], GROUP)

            def choose(n):
                step = [0]

                def done(ins):
                    step[0] += 1
                    ins.then_inc(s_top, 1)

                def wait():
                    dve.wait_ge(s_top, TOP_STEPS * n + step[0])

                def each(a):
                    return spread(a, [1, GROUP], [0, EXPERTS])

                def by_token(a):
                    return spread(a, [EXPERTS, GROUP], [1, EXPERTS])

                dve.wait_ge(s_logit, n + 1)
                logit = gbank[0][:, 0:GW]
                done(nc.vector.tensor_reduce(g_top[:, 0, :], by_token(logit), AX, ALU.max))
                wait()
                done(nc.vector.tensor_tensor(by_token(g_dif[:]), by_token(logit), each(g_top[:, 0, 0:1]),
                                             ALU.subtract))
                wait()
                for k, (src, sel) in enumerate(((g_dif, g_sel1), (g_sel2, g_sel2))):
                    if k == 1:
                        done(nc.vector.scalar_tensor_tensor(g_sel2[:], g_sel1[:], TAKEN, g_dif[:],
                                                            ALU.mult, ALU.add))
                        wait()
                        done(nc.vector.tensor_reduce(g_top[:, 2, :], by_token(g_sel2[:]), AX, ALU.max))
                        wait()
                        done(nc.vector.tensor_tensor(by_token(g_tmp[:]), by_token(g_sel2[:]),
                                                     each(g_top[:, 2, 0:1]), ALU.is_equal))
                        wait()
                        done(nc.vector.tensor_tensor(g_tmp[:], g_tmp[:], tie, ALU.mult))
                    else:
                        done(nc.vector.scalar_tensor_tensor(g_tmp[:], g_dif[:], 0.0, tie,
                                                            ALU.is_equal, ALU.mult))
                    wait()
                    done(nc.vector.tensor_reduce(g_top[:, 2 * k + 1, :], by_token(g_tmp[:]), AX, ALU.max))
                    wait()
                    done(nc.vector.tensor_tensor(by_token(sel[:]), by_token(g_tmp[:]),
                                                 each(g_top[:, 2 * k + 1, 0:1]), ALU.is_equal))
                    wait()
                done(nc.vector.tensor_tensor(g_sel1[:], g_sel1[:], g_sel2[:], ALU.add))
                assert step[0] == TOP_FIRST

            def weigh(n):
                step = [TOP_FIRST]

                def done(ins):
                    step[0] += 1
                    ins.then_inc(s_top, 1)

                def wait():
                    dve.wait_ge(s_top, TOP_STEPS * n + step[0])

                def by_token(a):
                    return spread(a, [EXPERTS, GROUP], [1, EXPERTS])

                wait()
                dve.wait_ge(s_gexp, n + 1)
                done(nc.vector.tensor_tensor(g_tmp[:], g_exp[:], g_sel1[:], ALU.mult))
                wait()
                done(nc.vector.tensor_reduce(g_sum[:], by_token(g_tmp[:]), AX, ALU.add))
                wait()
                done(nc.vector.reciprocal(g_rec[:], g_sum[:]))
                wait()
                done(nc.vector.tensor_tensor(by_token(g_sel2[:]), by_token(g_tmp[:]),
                                             spread(g_rec[:, 0:1], [1, GROUP], [0, EXPERTS]), ALU.mult))
                wait()
                if not isinstance(n, int) or n >= 1:
                    dve.wait_ge(s_gT, 2 * n)
                done(nc.vector.tensor_copy(gates[:, :, 0:EXPERTS], by_token(g_sel2[:])))
                wait()
                nc.vector.tensor_tensor(gates[:, :, EXPERTS:2 * EXPERTS], by_token(g_sel2[:]),
                                        gates[:, :, 0:EXPERTS].bitcast(f32), ALU.subtract)\
                    .then_inc(s_gate, 1)
                assert step[0] == TOP_STEPS

            def products(t, h):
                n, j = (t, GROUP - 1) if h == 0 or (isinstance(t, int) and t == GROUPS - 1) else (t + 1, REACH - 1)
                dve.wait_ge(s_front_free, front_base(n) + 2 + j + 1)
                if not isinstance(t, int) or t >= 1:
                    dve.wait_ge(s_oT, 2 * t + h - 1)
                slot = t * GROUP + h * HALF
                q = KV[:, bass.ds(slot, HALF), :]
                nc.vector.tensor_tensor(
                    spread(prod[h][:, 0, 0:1], [DIM, WINDOW], [WINDOW * DIM, HALF], [1, DIM]),
                    spread(q, [0, WINDOW], [DIM, HALF], [1, DIM]),
                    spread(windows(K0, slot), [DIM, WINDOW], [DIM, HALF], [1, DIM]),
                    ALU.mult).then_inc(s_qk, 1)

            def less_maximum(t, h, first, last):
                dve.wait_ge(s_score, 2 * t + h + 1)
                s = chain[h][:, 0:HALF * WH]
                masks = []
                if first and h == 0:
                    masks = [(j, 0, REACH - j, 0) for j in range(REACH)]
                if last and h == 1:
                    masks = [(HALF - 1 - i, WINDOW - REACH + i, WINDOW, 1) for i in range(REACH)]
                for i, (j, a, b, side) in enumerate(masks):
                    part = s[:, j * WH + a * HEADS:j * WH + b * HEADS]
                    ins = nc.vector.tensor_scalar(part, part, edge[side], None, ALU.add)
                    if i == len(masks) - 1:
                        ins.then_inc(s_mask, 1)
                        dve.wait_ge(s_mask, side + 1)
                nc.vector.tensor_reduce(
                    spread(smax[h][:, 0:1], [HEADS, HALF], [1, HEADS]),
                    spread(s, [WH, HALF], [1, HEADS], [HEADS, WINDOW]), AX, ALU.max).then_inc(s_max, 1)
                dve.wait_ge(s_max, 2 * t + h + 1)
                nc.vector.tensor_tensor(
                    spread(sc[h][:, 0, 0:1], [HW, WINDOW], [HEADS, HALF], [1, HEADS]),
                    spread(s, [HEADS, WINDOW], [WH, HALF], [1, HEADS]),
                    spread(smax[h][:, 0:1], [0, WINDOW], [HEADS, HALF], [1, HEADS]),
                    ALU.subtract).then_inc(s_dif, 1)

            def total(t, h):
                dve.wait_ge(s_exp, 2 * t + h + 1)
                nc.vector.tensor_reduce(ssum[h][:], spread(sc[h][:, 0, 0:1], [1, HW], [HW, WINDOW]),
                                        AX, ALU.add).then_inc(s_sum, 1)
                dve.wait_ge(s_sum, 2 * t + h + 1)
                nc.vector.reciprocal(srec[h][:], ssum[h][:]).then_inc(s_rec, 1)

            def weighted(t, h):
                dve.wait_ge(s_prob, 2 * t + h + 1)
                nc.vector.tensor_tensor(
                    spread(prod[h][:, 0, 0:1], [HD, WINDOW], [HEAD_DIM, HW], [1, HEAD_DIM]),
                    spread(sc[h][:, 0, 0:1], [HW, WINDOW], [1, HW], [0, HEAD_DIM]),
                    spread(windows(V0, t * GROUP + h * HALF), [DIM, WINDOW], [HEAD_DIM, HW], [1, HEAD_DIM]),
                    ALU.mult).then_inc(s_pv, 1)

            def gate(n, h):
                for m in range(CHUNKS):
                    i = h * CHUNKS + m
                    dve.wait_ge(s_front_free, front_base(n) + 2 + GROUP + i + 1)
                    dve.wait_ge(s_gb, 2 * CHUNKS * n + i + 1)
                    if m == 0 and (not isinstance(n, int) or n >= 1):
                        dve.wait_ge(s_w2, 2 * (n - 1) + h + 1)
                    nc.vector.tensor_tensor(hidg[:, h, m, :], hid[:, h, m, :], gbank[i % 2][:],
                                            ALU.mult).then_inc(s_hidg, 1)

            def result(t, h):
                dve.wait_ge(s_y, 2 * t + h + 1)
                dve.wait_ge(s_xb, t + 1)
                xs = X[:, bass.ds(t * GROUP + h * HALF, HALF), :]
                nc.vector.tensor_tensor(xs, xs, ybank[h][:].rearrange("p (j n) -> p j n", j=HALF),
                                        ALU.add).then_inc(s_res, 1)

            def body(t, attend=True, after=True, ahead=True, first=False, last=False):
                if attend:
                    products(t, 0)
                    if not first:
                        for h in range(2):
                            result(t - 1, h)
                    products(t, 1)
                if ahead:
                    group_statistics(t + 2)
                if after:
                    choose(t + 1)
                if attend:
                    for h in range(2):
                        less_maximum(t, h, first, last)
                if after:
                    weigh(t + 1)
                if attend:
                    for h in range(2):
                        total(t, h)
                for h in range(2):
                    if attend:
                        weighted(t, h)
                    if after:
                        gate(t + 1, h)

            dve.wait_ge(s_halo, 16 * 4)
            statistics(0, lambda j: XH[:, j, :], HALO)
            group_statistics(0)
            body(-1, attend=False)
            body(0, first=True)
            with dve.Fori(1, GROUPS - 2) as t:
                body(t)
            body(GROUPS - 2, ahead=False)
            body(GROUPS - 1, after=False, ahead=False, last=True)
            for h in range(2):
                result(GROUPS - 1, h)

        @block.tensor
        def _(pe):
            def rows_in(n, counts):
                pe.wait_ge(s_xn, n + 2)
                for h, count in enumerate(counts):
                    if not isinstance(n, int) or n >= 0:
                        pe.wait_ge(s_front_free, front_base(n) + h - 1)
                    for j in range(count):
                        last = nc.tensor.transpose(front[h][:, j * P:(j + 1) * P],
                                                   xn[:, h * HALF + j, :], ident)
                    last.then_inc(s_front, 1)

            def project(n, count, first):
                for j in range(count):
                    pe.wait_ge(s_front_free, front_base(n) + max(j, 1) + (j > 0))
                    bank = front[j % 2][:, first * DIM:3 * DIM]
                    nc.tensor.matmul(bank, ones_r[:], bias_r[:, first * DIM:3 * DIM],
                                     start=True, stop=False)
                    nc.tensor.matmul(bank, xnT[:, j, :], w_qkv[:, first:3, :],
                                     start=False, stop=True).then_inc(s_front, 1)

            def logits(n):
                if not isinstance(n, int) or n >= 1:
                    pe.wait_ge(s_hidg, 2 * CHUNKS * n - 1)
                nc.tensor.matmul(gbank[0][:, 0:GW], ones_r[:], bias_r[:, 3 * DIM:],
                                 start=True, stop=False, skip_group_check=True)
                for j in range(GROUP):
                    last = nc.tensor.matmul(gbank[0][:, j * EXPERTS:(j + 1) * EXPERTS], xnT[:, j, :],
                                            w_gate[:], start=False, stop=j == GROUP - 1,
                                            skip_group_check=True)
                last.then_inc(s_logit, 1)

            def scores_T(t, h):
                pe.wait_ge(s_qk, 2 * t + h + 1)
                if not isinstance(t, int) or t >= 1:
                    pe.wait_ge(s_oT_sb, 2 * t + h - 1)
                for j in range(HALF):
                    for d in range(HEAD_DIM):
                        p = bass.AP(prod[h][:].tensor, j * WINDOW * DIM + d,
                                    [list(prod[h][:].ap[0]), [HEAD_DIM, WH]])
                        last = nc.tensor.matmul(chain[h][0:WH, j * P:(j + 1) * P], p, ident,
                                                is_transpose=True, start=d == 0, stop=d == HEAD_DIM - 1)
                last.then_inc(s_scT, 1)

            def scores(t, h):
                pe.wait_ge(s_scT_sb, 2 * t + h + 1)
                for j in range(HALF):
                    last = nc.tensor.transpose(chain[h][:, j * WH:(j + 1) * WH],
                                               scT[h][0:WH, j * P:(j + 1) * P], ident[0:WH, 0:WH])
                last.then_inc(s_score, 1)

            def experts_out(t, h):
                pe.wait_ge(s_hidg, 2 * CHUNKS * t + (h + 1) * CHUNKS)
                if not isinstance(t, int) or t >= 1:
                    pe.wait_ge(s_res, 2 * t + h - 1)
                for j in range(HALF):
                    for m in range(CHUNKS):
                        last = nc.tensor.matmul(ybank[h][:, j * DIM:(j + 1) * DIM],
                                                hidg[:, h, m, j * P:(j + 1) * P], w2_sb[:, m, :],
                                                start=j == 0 and m == 0, stop=False,
                                                skip_group_check=True)
                last.then_inc(s_w2, 1)

            def hidden(n, h):
                for m in range(CHUNKS):
                    i = h * CHUNKS + m
                    pe.wait_ge(s_front_free, front_base(n) + 2 + GROUP + i - 1)
                    nc.tensor.matmul(front[i % 2][:], w1_sb[:, m * P:(m + 1) * P],
                                     xnT[:, h * HALF:(h + 1) * HALF, :],
                                     start=True, stop=True).then_inc(s_front, 1)

            def gates_T(n):
                pe.wait_ge(s_gate, n + 1)
                if not isinstance(n, int) or n >= 1:
                    pe.wait_ge(s_hidg, 2 * CHUNKS * n)
                for h in range(2):
                    for j in range(HALF):
                        last = nc.tensor.transpose(gbank[h][0:2 * EXPERTS, j * P:(j + 1) * P],
                                                   gates[:, h * HALF + j, :].bitcast(f32), ident)
                    last.then_inc(s_gT, 1)

            def gates_spread(n, h, ms):
                for m in ms:
                    i = h * CHUNKS + m
                    if i < 2:
                        pe.wait_ge(s_gT_sb, 2 * n + 2)
                    else:
                        pe.wait_ge(s_hidg, 2 * CHUNKS * n + i - 1)
                    nc.tensor.matmul(gbank[i % 2][:], sel_r[:, m * P:(m + 1) * P],
                                     gT[:, h * HD:(h + 1) * HD], start=True, stop=True)\
                        .then_inc(s_gb, 1)

            def attention_out(t, h):
                pe.wait_ge(s_pv, 2 * t + h + 1)
                for j in range(HALF):
                    for k in range(WINDOW):
                        last = nc.tensor.matmul(chain[h][:, j * P:(j + 1) * P],
                                                prod[h][:, k, j * DIM:(j + 1) * DIM], ident,
                                                is_transpose=True, start=k == 0, stop=k == WINDOW - 1)
                last.then_inc(s_oT, 1)
                return last

            def project_out(t, h):
                pe.wait_ge(s_oT_sb, 2 * t + h + 1)
                for j in range(HALF):
                    last = nc.tensor.matmul(ybank[h][:, j * DIM:(j + 1) * DIM],
                                            oT_sb[h][:, j * P:(j + 1) * P], w_out[:],
                                            start=False, stop=True, skip_group_check=True)
                last.then_inc(s_y, 1)

            def body(t, attend=True, after=True):
                u = t + 1
                if after:
                    rows_in(u, (HALF, HALF))
                    project(u, GROUP, 0)
                    logits(u)
                if attend:
                    for h in range(2):
                        scores_T(t, h)
                    for h in range(2):
                        scores(t, h)
                if after:
                    hidden(u, 0)
                if attend:
                    experts_out(t, 0)
                if after:
                    gates_T(u)
                    gates_spread(u, 0, (0, 1))
                    hidden(u, 1)
                if attend:
                    attention_out(t, 0)
                    project_out(t, 0)
                if after:
                    gates_spread(u, 0, (2, 3))
                if attend:
                    experts_out(t, 1)
                if after:
                    gates_spread(u, 1, (0, 1))
                if attend:
                    attention_out(t, 1)
                    project_out(t, 1)
                if after:
                    gates_spread(u, 1, (2, 3))

            pe.wait_ge(s_const, 16 * 11)
            pe.wait_ge(s_prep, 5)
            rows_in(-1, (HALF, HALO - HALF))
            pe.wait_ge(s_wproj, 16 * 4)
            project(-1, HALO, 1)
            pe.wait_ge(s_wffn, 16 * 3)
            body(-1, attend=False)
            body(0)
            with pe.Fori(1, GROUPS - 1) as t:
                body(t)
            body(GROUPS - 1, after=False)


TOP_FIRST = 12
TOP_STEPS = 17

_INS = ['L0_attn_hidden_states', 'L0_attn_w_q', 'L0_attn_b_q', 'L0_attn_w_k', 'L0_attn_b_k',
        'L0_attn_w_v', 'L0_attn_b_v', 'L0_attn_w_o', 'L0_attn_b_o', 'L0_ffn_Wg', 'L0_ffn_bg',
        'L0_ffn_W1', 'L0_ffn_W2']


def kernel(**inputs):
    import numpy as _np
    import concourse.bacc as _bacc
    from concourse import mybir as _mybir
    from concourse.bass_utils import run_bass_kernel_spmd as _run

    nc = _bacc.Bacc("TRN2", target_bir_lowering=False, num_devices=1)
    layout = {
        'L0_ffn_Wg': lambda a: a.T,
        'L0_ffn_W1': lambda a: a.reshape(EXPERTS * RANK, DIM).T,
        'L0_ffn_W2': lambda a: a.transpose(0, 2, 1).reshape(EXPERTS * RANK, DIM),
    }
    arrays, args = {}, []
    for name in _INS:
        a = _np.asarray(inputs[name])
        a = _np.ascontiguousarray(layout[name](a) if name in layout else a)
        arrays[f"in_{name}_dram"] = a
        args.append(nc.dram_tensor(f"in_{name}_dram", a.shape, _mybir.dt.from_np(a.dtype), kind="ExternalInput").ap())
    arrays["in_const_dram"] = constants()
    args.append(nc.dram_tensor("in_const_dram", (P, C_ALL), _mybir.dt.float32, kind="ExternalInput").ap())
    args.append(nc.dram_tensor("out_0_dram", (BATCH, SEQ, DIM), _mybir.dt.float32, kind="ExternalOutput").ap())
    attention_and_experts(nc, *args)
    r = _run(nc, [arrays], core_ids=[0])
    return r.results[0]["out_0_dram"]
```

```python
import numpy as np
import concourse.bass as bass
from concourse import mybir
from contextlib import ExitStack

BATCH, SEQ, DIM = 16, 512, 128
HEADS, HEAD_DIM = 16, 8
WINDOW, REACH = 7, 3
EXPERTS, RANK = 8, 64
SCALING = 128.0 / RANK
SCALE = HEAD_DIM ** -0.5
EPS = 1e-5
P = 128

TOKENS = BATCH * SEQ
PER = TOKENS // P
PARTS = SEQ // PER
HALO = 2 * REACH
SLOTS = PER + HALO
GROUP = 8
GROUPS = PER // GROUP
HALF = GROUP // 2
V0 = 3 * GROUP
K0 = V0 + 3 * GROUP + REACH
PLACES = K0 + SLOTS
HD = HALF * DIM
WH = WINDOW * HEADS
HW = HALF * HEADS
CHUNKS = EXPERTS * RANK // P
PER_CHUNK = P // RANK
GW = GROUP * EXPERTS

C_IDENT = 0
C_TIE = C_IDENT + P
C_EDGE = C_TIE + GW
C_NORM = C_EDGE + 2
NORM_CONSTANTS = (DIM / 4, 1 / DIM, EPS, -0.5)
C_KEEP = C_NORM + GROUP * len(NORM_CONSTANTS)
C_SEL = C_KEEP
C_ONES = C_SEL + CHUNKS * P
C_ALL = C_ONES + P
NEVER = -1e30
TAKEN = -3e38

W_ALL = 3 * DIM + EXPERTS
B_PROJ = W_ALL - DIM
B_ALL = B_PROJ + DIM

NORM_STEPS = 10
TOP_FIRST, TOP_STEPS = 12, 17


def constants():
    c = np.zeros((P, C_ALL), np.float32)
    c[:, C_IDENT:C_IDENT + P] = np.eye(P)
    c[:, C_TIE:C_TIE + GW] = np.tile(np.arange(EXPERTS, 0, -1), GROUP)
    for m in range(CHUNKS):
        for r in range(P):
            for part in range(2):
                c[EXPERTS * part + m * PER_CHUNK + r // RANK, C_SEL + m * P + r] = SCALING
    c[0, C_ONES:C_ONES + P] = 1.0
    c[32, C_ONES:C_ONES + P] = 1.0
    c[0::PARTS, C_EDGE] = NEVER
    c[PARTS - 1::PARTS, C_EDGE + 1] = NEVER
    for i, value in enumerate(NORM_CONSTANTS):
        c[:, C_NORM + i * GROUP:C_NORM + (i + 1) * GROUP] = value
    return c


def past(n, least):
    return not isinstance(n, int) or n >= least


def active(n):
    return not isinstance(n, int) or 0 <= n < GROUPS


def projected(n, j):
    return HALO + n * GROUP + j + 1


def attention_and_experts(nc, x, w_proj, b_proj, bv, wo, bo, w1, w2, const, out):
    f32, f32r = mybir.dt.float32, mybir.dt.float32r
    ALU, ACT, AX = mybir.AluOpType, mybir.ActivationFunctionType, mybir.AxisListType.X
    x_tok = x.rearrange("b s h -> (b s) h")
    x_view = x_tok.rearrange("(p j) h -> p j h", j=PER)
    out_view = out.rearrange("b s h -> (b s) h").rearrange("(p j) h -> p j h", j=PER)

    with ExitStack() as ctx:
        def sb(name, shape, dt=f32):
            return ctx.enter_context(nc.sbuf_tensor(name, shape, dt))

        def pb(name):
            return ctx.enter_context(nc.psum_tensor(name, [P, 512], f32))

        def sem(name):
            return ctx.enter_context(nc.semaphore(name))

        X = sb("X", [P, PER, DIM])
        KV = sb("KV", [P, PLACES, DIM])
        KV_end = sb("KV_end", [P, 2, REACH, DIM])
        const_sb = sb("const_sb", [P, C_KEEP])
        wp_hi, wp_lo = (sb(f"wp_{x}", [P, W_ALL], f32r) for x in ("hi", "lo"))
        w1_hi, w1_lo = (sb(f"w1_{x}", [P, CHUNKS * P], f32r) for x in ("hi", "lo"))
        w_out = sb("w_out", [P, DIM])
        w2_sb = sb("w2_sb", [P, CHUNKS, DIM])
        bias_r = sb("bias_r", [64, B_ALL], f32r)
        ones_r = sb("ones_r", [64, P], f32r)
        sel_r = sb("sel_r", [64, CHUNKS * P], f32r)
        st6 = sb("st6", [P, GROUP, 6])
        n_mean = sb("n_mean", [P, GROUP])
        dif = sb("dif", [P, GROUP])
        rstd = sb("rstd", [P, GROUP])
        shift = sb("shift", [P, GROUP])
        xn = sb("xn", [P, GROUP, DIM])
        x_hi = sb("x_hi", [P, GROUP, P], f32r)
        x_lo = sb("x_lo", [P, GROUP, P], f32r)
        prod = [sb(f"prod{h}", [P, WINDOW, HD]) for h in range(2)]
        sc = [sb(f"sc{h}", [P, WINDOW, HW]) for h in range(2)]
        smax = [sb(f"smax{h}", [P, HW]) for h in range(2)]
        srec = [sb(f"srec{h}", [P, HW]) for h in range(2)]
        ssum = [sb(f"ssum{h}", [P, HW]) for h in range(2)]
        scT = sb("scT", [P, HD])
        oT_sb = [sb(f"oT_sb{h}", [P, HD]) for h in range(2)]
        hid = sb("hid", [P, 2 * CHUNKS, HD])
        hidg = sb("hidg", [P, 2 * CHUNKS, HD])
        logit = sb("logit", [P, GROUP, EXPERTS])
        g_top = sb("g_top", [P, 4, GROUP])
        g_dif = sb("g_dif", [P, GW])
        g_tmp = sb("g_tmp", [P, GW])
        g_sel1 = sb("g_sel1", [P, GW])
        g_sel2 = sb("g_sel2", [P, GW])
        g_exp = sb("g_exp", [P, GW])
        g_sum = sb("g_sum", [P, GROUP])
        g_rec = sb("g_rec", [P, GROUP])
        gates = sb("gates", [P, GROUP, 2 * EXPERTS], f32r)
        gT = sb("gT", [64, GROUP * P], f32r)

        early_at = [0]

        def early(rows, *shape):
            steps, size = [], 1
            for n in reversed(shape):
                steps.insert(0, [size, n])
                size *= n
            a = bass.AP(prod[0][:].tensor, early_at[0], [[prod[0][:].ap[0][0], rows], *steps])
            early_at[0] += size
            assert early_at[0] <= WINDOW * HD
            return a

        XH = early(P, HALO, DIM)
        wp_raw = early(P, W_ALL)
        w1_raw = early(P, CHUNKS * P)
        const_raw = early(64, C_ALL - C_KEEP)
        bias_raw = early(64, B_ALL)
        bias_hi = early(64, B_ALL).bitcast(f32r)
        bv_col = early(P, 1)
        bv_rep = early(P, 64)

        front = [pb("front0"), pb("front1")]
        gbank = [pb("gbank0"), pb("gbank1")]
        chain = [pb("chain0"), pb("chain1")]
        rounds = [front[0], front[1], chain[1]]
        ybank = [pb("ybank0"), pb("ybank1")]

        ident = const_sb[:, C_IDENT:C_IDENT + P]
        tie = const_sb[:, C_TIE:C_TIE + GW]
        edge = [const_sb[:, C_EDGE:C_EDGE + 1], const_sb[:, C_EDGE + 1:C_EDGE + 2]]
        quarter_dim, per_dim, eps, minus_half = (
            const_sb[:, C_NORM + i * GROUP:C_NORM + (i + 1) * GROUP] for i in range(len(NORM_CONSTANTS)))

        s_const = sem("s_const")
        s_bias = sem("s_bias")
        s_wp = sem("s_wp")
        s_w1 = sem("s_w1")
        s_w2in = sem("s_w2in")
        s_halo0 = sem("s_halo0")
        s_halo = sem("s_halo")
        s_x = sem("s_x")
        s_zero = sem("s_zero")
        s_prep = sem("s_prep")
        s_bvo = sem("s_bvo")
        s_stat = sem("s_stat")
        s_rstd = sem("s_rstd")
        s_norm = sem("s_norm")
        s_xn = sem("s_xn")
        s_xT = sem("s_xT")
        s_xhi = sem("s_xhi")
        s_xlo = sem("s_xlo")
        s_qkv = sem("s_qkv")
        s_qkv_sb = sem("s_qkv_sb")
        s_top = sem("s_top")
        s_gexp = sem("s_gexp")
        s_gate = sem("s_gate")
        s_gT = sem("s_gT")
        s_gT_sb = sem("s_gT_sb")
        s_gb = sem("s_gb")
        s_h = sem("s_h")
        s_hid = sem("s_hid")
        s_hidg = sem("s_hidg")
        s_qk = sem("s_qk")
        s_scT = sem("s_scT")
        s_scT_sb = sem("s_scT_sb")
        s_score = [sem("s_score0"), sem("s_score1")]
        s_mask = sem("s_mask")
        s_max = sem("s_max")
        s_dif = sem("s_dif")
        s_exp = sem("s_exp")
        s_sum = sem("s_sum")
        s_rec = sem("s_rec")
        s_prob = sem("s_prob")
        s_pv = sem("s_pv")
        s_oT = sem("s_oT")
        s_oT_sb = sem("s_oT_sb")
        s_w2 = sem("s_w2")
        s_y = sem("s_y")
        s_res = sem("s_res")
        s_store = sem("s_store")

        def windows(place, first):
            a = KV[:, bass.ds(first + place, HALF), :]
            return bass.AP(a.tensor, a.offset, [list(a.ap[0]), [DIM, WINDOW], [1, HD]])

        def spread(a, *dims):
            return bass.AP(a.tensor, a.offset, [list(a.ap[0]), *map(list, dims)])


        block = ctx.enter_context(nc.Block())

        @block.sync
        def _(sp):
            sp.wait_ge(s_halo0, 1)
            for a, b in ((1, 16), (16, P)):
                src = x_tok[a * PER - REACH:b * PER - REACH, :].rearrange("(p j) h -> p j h", j=PER)
                sp.dma_start(XH[a:b, 0:REACH, :], src[:, 0:REACH, :]).then_inc(s_halo, 16)
            for a, b in ((0, P - 16), (P - 16, P - 1)):
                src = x_tok[(a + 1) * PER:(b + 1) * PER, :].rearrange("(p j) h -> p j h", j=PER)
                sp.dma_start(XH[a:b, REACH:HALO, :], src[:, 0:REACH, :]).then_inc(s_halo, 16)
            sp.dma_start(X[:, 0:GROUP, :], x_view[:, 0:GROUP, :]).then_inc(s_x, 16)
            with sp.Fori(1, GROUPS) as n:
                sp.wait_ge(s_x, 16 * n)
                sp.dma_start(X[:, bass.ds(n * GROUP, GROUP), :],
                             x_view[:, bass.ds(n * GROUP, GROUP), :]).then_inc(s_x, 16)
            with sp.Fori(0, GROUPS) as n:
                sp.wait_ge(s_res, 2 * n + 2)
                sp.dma_start(out_view[:, bass.ds(n * GROUP, GROUP), :],
                             X[:, bass.ds(n * GROUP, GROUP), :]).then_inc(s_store, 16)
            sp.wait_ge(s_store, 16 * GROUPS)

        @block.gpsimd
        def _(pool):
            nc.gpsimd.memset(XH, 0.0).then_inc(s_halo0, 1)
            pool.wait_ge(s_const, 16)

            def scale_and_shift(stage, count):
                step = [0]

                def op(out, in0, in1, alu):
                    step[0] += 1
                    nc.gpsimd.tensor_tensor(out, in0, in1, alu).then_inc(s_rstd, 1)

                def wait():
                    pool.wait_ge(s_rstd, NORM_STEPS * stage + step[0])

                def col(a):
                    return a[:, 0:count]

                pool.wait_ge(s_stat, stage + 1)
                op(col(n_mean), st6[:, 0:count, 1], st6[:, 0:count, 4], ALU.add)
                op(col(dif), st6[:, 0:count, 1], st6[:, 0:count, 4], ALU.subtract)
                if past(stage, 1):
                    pool.wait_ge(s_xn, stage)
                op(col(rstd), st6[:, 0:count, 2], st6[:, 0:count, 5], ALU.add)
                wait()
                op(col(dif), col(dif), col(dif), ALU.mult)
                wait()
                op(col(dif), col(dif), col(quarter_dim), ALU.mult)
                wait()
                op(col(rstd), col(rstd), col(dif), ALU.add)
                wait()
                op(col(rstd), col(rstd), col(per_dim), ALU.mult)
                op(col(n_mean), col(n_mean), col(minus_half), ALU.mult)
                wait()
                op(col(rstd), col(rstd), col(eps), ALU.add)
                wait()
                op(col(rstd), col(rstd), col(minus_half), ALU.pow)
                wait()
                nc.gpsimd.tensor_tensor(col(shift), col(n_mean), col(rstd), ALU.mult)\
                    .then_inc(s_norm, 1)
                assert step[0] == NORM_STEPS

            def probabilities(t, h):
                pool.wait_ge(s_rec, 2 * t + h + 1)
                nc.gpsimd.tensor_tensor(sc[h][:], sc[h][:],
                                        spread(srec[h][:, 0:1], [0, WINDOW], [1, HW]),
                                        ALU.mult).then_inc(s_prob, 1)

            def body(t):
                if active(t + 3):
                    scale_and_shift(t + 4, GROUP)
                if active(t):
                    for h in range(2):
                        probabilities(t, h)

            scale_and_shift(0, HALO)
            scale_and_shift(1, GROUP)
            for t in (-2, -1, 0):
                body(t)
            with pool.Fori(1, GROUPS - 3) as t:
                body(t)
            for t in (GROUPS - 3, GROUPS - 2, GROUPS - 1):
                body(t)
        @block.scalar
        def _(act):
            act.dma_start(const_sb[:], const[:, 0:C_KEEP]).then_inc(s_const, 16)
            act.dma_start(wp_raw, w_proj).then_inc(s_wp, 16)
            act.dma_start(bias_raw[:, 0:B_PROJ], b_proj).then_inc(s_bias, 16)
            act.dma_start(bias_raw[:, B_PROJ:], bo.rearrange("(a n) -> a n", a=1).broadcast_to([64, DIM]))\
                .then_inc(s_bias, 16)
            act.dma_start(const_raw, const[0:64, C_KEEP:C_ALL]).then_inc(s_bias, 16)
            act.dma_start(bv_col, bv.rearrange("(p a) -> p a", a=1)).then_inc(s_bias, 16)
            act.dma_start(w1_raw, w1).then_inc(s_w1, 16)
            act.dma_start(w_out[:], wo).then_inc(s_w2in, 16)
            act.dma_start(w2_sb[:], w2.rearrange("(c p) n -> p c n", p=P)).then_inc(s_w2in, 16)

            def normalise(stage, row, count):
                act.wait_ge(s_norm, stage + 1)
                if past(stage, 1):
                    act.wait_ge(s_xT, 2 * stage)
                for j in range(count):
                    last = act.activation(xn[:, j, :], row(j), ACT.Identity,
                                          bias=shift[:, j:j + 1], scale=rstd[:, j:j + 1])
                last.then_inc(s_xn, 1)

            def group_normalise(n):
                normalise(n + 1, lambda j: X[:, bass.ds(n * GROUP + j, 1), :], GROUP)

            def high_part(stage, counts):
                for h, count in enumerate(counts):
                    act.wait_ge(s_xT, 2 * stage + h + 1)
                    act.activation(x_hi[:, h * HALF:h * HALF + count, :],
                                   front[h][:, 0:count * P], ACT.Copy).then_inc(s_xhi, 1)

            def halo_in():
                for j in range(HALO):
                    act.wait_ge(s_qkv, j + 1)
                    if j < REACH:
                        dst = spread(KV[:, V0 + j, 0:1], [(K0 - V0) * DIM, 2], [1, DIM])
                    else:
                        dst = KV_end[:, :, j - REACH, :]
                    act.activation(dst, rounds[j % 3][:, 0:2 * DIM].rearrange("p (c n) -> p c n", c=2),
                                   ACT.Copy).then_inc(s_qkv_sb, 1)

            def group_in(n):
                for j in range(GROUP):
                    act.wait_ge(s_qkv, projected(n, j))
                    if j == 0 and past(n, 3):
                        act.wait_ge(s_pv, 2 * n - 4)
                        act.wait_ge(s_qk, 2 * n - 4)
                    v = KV[:, bass.ds(n * GROUP + (V0 + REACH + j), 1), :]
                    act.activation(spread(v, [(K0 - V0) * DIM, 2], [1, DIM]),
                                   rounds[j % 3][:, 0:2 * DIM].rearrange("p (c n) -> p c n", c=2), ACT.Copy)
                    act.activation(KV[:, bass.ds(n * GROUP + j, 1), :],
                                   rounds[j % 3][:, 2 * DIM:3 * DIM], ACT.Copy)
                    if j == 0 and past(n, 1):
                        act.wait_ge(s_top, TOP_STEPS * (n - 1) + 2)
                    act.activation(logit[:, j, :], rounds[j % 3][:, 3 * DIM:W_ALL], ACT.Copy)\
                        .then_inc(s_qkv_sb, 1)

            def hidden(n, chunks):
                for i in chunks:
                    act.wait_ge(s_h, 2 * CHUNKS * n + i + 1)
                    if past(n, 1):
                        act.wait_ge(s_hidg, 2 * CHUNKS * (n - 1) + i + 1)
                    act.activation(hid[:, i, :], rounds[i % 3][:], ACT.Gelu).then_inc(s_hid, 1)

            def gates_in(n):
                if past(n, 1):
                    act.wait_ge(s_gb, 2 * CHUNKS * n)
                for h in range(2):
                    act.wait_ge(s_gT, 2 * n + h + 1)
                    act.activation(gT[0:2 * EXPERTS, h * HD:(h + 1) * HD],
                                   gbank[h][0:2 * EXPERTS, :], ACT.Copy).then_inc(s_gT_sb, 1)

            def exponentials(t, h):
                act.wait_ge(s_dif, 2 * t + h + 1)
                act.activation(sc[h][:], sc[h][:], ACT.Exp, scale=SCALE).then_inc(s_exp, 1)

            def attention_in(t, h):
                act.wait_ge(s_oT, 2 * t + h + 1)
                act.activation(oT_sb[h][:], chain[h][:], ACT.Copy).then_inc(s_oT_sb, 1)

            def gate_exp(n):
                act.wait_ge(s_top, TOP_STEPS * n + 2)
                if past(n, 1):
                    act.wait_ge(s_gate, n)
                act.activation(g_exp[:], g_dif[:], ACT.Exp).then_inc(s_gexp, 1)

            def scores_in(t):
                act.wait_ge(s_scT, t + 1)
                act.activation(scT[0:WH, :], chain[0][0:WH, :], ACT.Copy).then_inc(s_scT_sb, 1)

            def halo_end_in():
                act.wait_ge(s_qk, 2 * (GROUPS - 2))
                end = spread(KV[:, V0 + REACH + PER, 0:1], [(K0 - V0) * DIM, 2], [1, REACH * DIM])
                act.activation(end, KV_end[:].rearrange("p c j n -> p c (j n)"), ACT.Copy)\
                    .then_inc(s_qkv_sb, 1)

            def body(t):
                if active(t + 1):
                    gate_exp(t + 1)
                if active(t) and past(t, 1):
                    attention_in(t - 1, 1)
                if active(t):
                    scores_in(t)
                if active(t + 2):
                    group_normalise(t + 2)
                if active(t):
                    for h in range(2):
                        exponentials(t, h)
                if active(t + 1):
                    gates_in(t + 1)
                    hidden(t + 1, range(2 * CHUNKS))
                if active(t + 2):
                    high_part(t + 3, (HALF, HALF))
                if active(t):
                    attention_in(t, 0)
                if active(t + 2):
                    group_in(t + 2)
                elif t + 2 == GROUPS:
                    halo_end_in()

            normalise(0, lambda j: XH[:, j, :], HALO)
            high_part(0, (HALF, HALO - HALF))
            halo_in()
            for t in (-2, -1, 0):
                body(t)
            with act.Fori(1, GROUPS - 3) as t:
                body(t)
            for t in (GROUPS - 3, GROUPS - 2, GROUPS - 1):
                body(t)
            attention_in(GROUPS - 1, 1)

        @block.vector
        def _(dve):
            nc.vector.memset(bias_r[:].bitcast(f32), 0.0).then_inc(s_zero, 1)
            nc.vector.memset(gT[:].bitcast(f32), 0.0).then_inc(s_zero, 1)

            def low_part(stage, counts):
                for h, count in enumerate(counts):
                    dve.wait_ge(s_xhi, 2 * stage + h + 1)
                    rows = slice(h * HALF, h * HALF + count)
                    nc.vector.tensor_tensor(x_lo[:, rows, :],
                                            front[h][:, 0:count * P].rearrange("p (j n) -> p j n", n=P),
                                            x_hi[:, rows, :].bitcast(f32), ALU.subtract).then_inc(s_xlo, 1)

            def result(t, h):
                dve.wait_ge(s_y, 2 * t + h + 1)
                xs = X[:, bass.ds(t * GROUP + h * HALF, HALF), :]
                nc.vector.tensor_tensor(xs, xs, ybank[h][:].rearrange("p (j n) -> p j n", j=HALF),
                                        ALU.add).then_inc(s_res, 1)

            def statistics(stage, row, count):
                if past(stage, 1):
                    dve.wait_ge(s_norm, stage)
                for j in range(count):
                    last = nc.vector.bn_stats(st6[:, j, :], row(j))
                    yield
                last.then_inc(s_stat, 1)

            def group_statistics(n):
                dve.wait_ge(s_x, 16 * (n + 1))
                yield from statistics(n + 1, lambda j: X[:, bass.ds(n * GROUP + j, 1), :], GROUP)

            def choose(n, between):
                step = [0]

                def done(ins):
                    step[0] += 1
                    ins.then_inc(s_top, 1)
                    between()
                    dve.wait_ge(s_top, TOP_STEPS * n + step[0])

                def each(i):
                    return spread(g_top[:, i, 0:1], [1, GROUP], [0, EXPERTS])

                def by_token(a):
                    return spread(a, [EXPERTS, GROUP], [1, EXPERTS])

                dve.wait_ge(s_qkv_sb, projected(n, GROUP - 1))
                done(nc.vector.tensor_reduce(g_top[:, 0, :], logit[:], AX, ALU.max))
                done(nc.vector.tensor_tensor(by_token(g_dif[:]), logit[:], each(0), ALU.subtract))
                done(nc.vector.scalar_tensor_tensor(g_tmp[:], g_dif[:], 0.0, tie, ALU.is_equal, ALU.mult))
                done(nc.vector.tensor_reduce(g_top[:, 1, :], by_token(g_tmp[:]), AX, ALU.max))
                done(nc.vector.tensor_tensor(by_token(g_sel1[:]), by_token(g_tmp[:]), each(1), ALU.is_equal))
                done(nc.vector.scalar_tensor_tensor(g_sel2[:], g_sel1[:], TAKEN, g_dif[:], ALU.mult, ALU.add))
                done(nc.vector.tensor_reduce(g_top[:, 2, :], by_token(g_sel2[:]), AX, ALU.max))
                done(nc.vector.tensor_tensor(by_token(g_tmp[:]), by_token(g_sel2[:]), each(2), ALU.is_equal))
                done(nc.vector.tensor_tensor(g_tmp[:], g_tmp[:], tie, ALU.mult))
                done(nc.vector.tensor_reduce(g_top[:, 3, :], by_token(g_tmp[:]), AX, ALU.max))
                done(nc.vector.tensor_tensor(by_token(g_sel2[:]), by_token(g_tmp[:]), each(3), ALU.is_equal))
                done(nc.vector.tensor_tensor(g_sel1[:], g_sel1[:], g_sel2[:], ALU.add))
                assert step[0] == TOP_FIRST

            def weigh(n):
                step = [TOP_FIRST]

                def done(ins):
                    step[0] += 1
                    ins.then_inc(s_top, 1)
                    dve.wait_ge(s_top, TOP_STEPS * n + step[0])

                def by_token(a):
                    return spread(a, [EXPERTS, GROUP], [1, EXPERTS])

                dve.wait_ge(s_gexp, n + 1)
                done(nc.vector.tensor_tensor(g_tmp[:], g_exp[:], g_sel1[:], ALU.mult))
                done(nc.vector.tensor_reduce(g_sum[:], by_token(g_tmp[:]), AX, ALU.add))
                done(nc.vector.reciprocal(g_rec[:], g_sum[:]))
                done(nc.vector.tensor_tensor(by_token(g_sel2[:]), by_token(g_tmp[:]),
                                             spread(g_rec[:, 0:1], [1, GROUP], [0, EXPERTS]), ALU.mult))
                if past(n, 1):
                    dve.wait_ge(s_gT, 2 * n)
                done(nc.vector.tensor_copy(gates[:, :, 0:EXPERTS], by_token(g_sel2[:])))
                nc.vector.tensor_tensor(gates[:, :, EXPERTS:2 * EXPERTS], by_token(g_sel2[:]),
                                        gates[:, :, 0:EXPERTS].bitcast(f32), ALU.subtract)\
                    .then_inc(s_gate, 1)
                assert step[0] == TOP_STEPS

            def products(t, h):
                if h == 0:
                    dve.wait_ge(s_qkv_sb, projected(t, GROUP - 1))
                else:
                    dve.wait_ge(s_qkv_sb, projected(t + 1, REACH - 1 if active(t + 1) else 0))
                if past(t, 1):
                    dve.wait_ge(s_oT, 2 * t + h - 1)
                slot = t * GROUP + h * HALF
                q = KV[:, bass.ds(slot, HALF), :]
                nc.vector.tensor_tensor(
                    spread(prod[h][:, 0, 0:1], [DIM, WINDOW], [WINDOW * DIM, HALF], [1, DIM]),
                    spread(q, [0, WINDOW], [DIM, HALF], [1, DIM]),
                    spread(windows(K0, slot), [DIM, WINDOW], [DIM, HALF], [1, DIM]),
                    ALU.mult).then_inc(s_qk, 1)

            def scores(t):
                dve.wait_ge(s_qk, 2 * t + 2)
                if past(t, 1):
                    dve.wait_ge(s_oT_sb, 2 * t)
                nc.vector.tensor_reduce(chain[1][:, 0:HALF * WH],
                                        spread(prod[1][:, 0, 0:1], [HEAD_DIM, HALF * WH], [1, HEAD_DIM]),
                                        AX, ALU.add).then_inc(s_score[1], 1)

            def less_maximum(t, h):
                dve.wait_ge(s_score[h], t + 1)
                s = chain[h][:, 0:HALF * WH]
                masks = []
                if isinstance(t, int) and t == 0 and h == 0:
                    masks = [(j, 0, REACH - j, 0) for j in range(REACH)]
                if not active(t + 1) and h == 1:
                    masks = [(HALF - 1 - i, WINDOW - REACH + i, WINDOW, 1) for i in range(REACH)]
                for i, (j, a, b, side) in enumerate(masks):
                    part = s[:, j * WH + a * HEADS:j * WH + b * HEADS]
                    ins = nc.vector.tensor_scalar(part, part, edge[side], None, ALU.add)
                    if i == len(masks) - 1:
                        ins.then_inc(s_mask, 1)
                        dve.wait_ge(s_mask, side + 1)
                nc.vector.tensor_reduce(
                    spread(smax[h][:, 0:1], [HEADS, HALF], [1, HEADS]),
                    spread(s, [WH, HALF], [1, HEADS], [HEADS, WINDOW]), AX, ALU.max).then_inc(s_max, 1)
                dve.wait_ge(s_max, 2 * t + h + 1)
                nc.vector.tensor_tensor(
                    spread(sc[h][:, 0, 0:1], [HW, WINDOW], [HEADS, HALF], [1, HEADS]),
                    spread(s, [HEADS, WINDOW], [WH, HALF], [1, HEADS]),
                    spread(smax[h][:, 0:1], [0, WINDOW], [HEADS, HALF], [1, HEADS]),
                    ALU.subtract).then_inc(s_dif, 1)

            def total(t, h):
                dve.wait_ge(s_exp, 2 * t + h + 1)
                nc.vector.tensor_reduce(ssum[h][:], spread(sc[h][:, 0, 0:1], [1, HW], [HW, WINDOW]),
                                        AX, ALU.add).then_inc(s_sum, 1)
                dve.wait_ge(s_sum, 2 * t + h + 1)
                nc.vector.reciprocal(srec[h][:], ssum[h][:]).then_inc(s_rec, 1)

            def weighted(t, h):
                dve.wait_ge(s_prob, 2 * t + h + 1)
                nc.vector.tensor_tensor(
                    spread(prod[h][:, 0, 0:1], [HD, WINDOW], [HEAD_DIM, HW], [1, HEAD_DIM]),
                    spread(sc[h][:, 0, 0:1], [HW, WINDOW], [1, HW], [0, HEAD_DIM]),
                    spread(windows(V0, t * GROUP + h * HALF), [DIM, WINDOW], [HEAD_DIM, HW], [1, HEAD_DIM]),
                    ALU.mult).then_inc(s_pv, 1)

            def gate(n, pair):
                for i in (2 * pair, 2 * pair + 1):
                    dve.wait_ge(s_hid, 2 * CHUNKS * n + i + 1)
                    dve.wait_ge(s_gb, 2 * CHUNKS * n + i + 1)
                    if i % CHUNKS == 0 and past(n, 1):
                        dve.wait_ge(s_w2, 2 * (n - 1) + i // CHUNKS + 1)
                    nc.vector.tensor_tensor(hidg[:, i, :], hid[:, i, :], gbank[i % 2][:],
                                            ALU.mult).then_inc(s_hidg, 1)

            def body(t):
                if active(t):
                    products(t, 0)
                rest = group_statistics(t + 3) if active(t + 3) else iter(())
                if active(t + 1):
                    choose(t + 1, lambda: next(rest, None))
                for _ in rest:
                    pass
                if active(t):
                    products(t, 1)
                    if past(t, 1):
                        result(t - 1, 0)
                        result(t - 1, 1)
                if active(t + 1):
                    weigh(t + 1)
                if active(t):
                    scores(t)
                    less_maximum(t, 0)
                    less_maximum(t, 1)
                    total(t, 0)
                    total(t, 1)
                if active(t + 1):
                    gate(t + 1, 0)
                if active(t):
                    weighted(t, 0)
                if active(t + 1):
                    gate(t + 1, 1)
                    gate(t + 1, 2)
                if active(t + 2):
                    low_part(t + 3, (HALF, HALF))
                if active(t):
                    weighted(t, 1)
                if active(t + 1):
                    gate(t + 1, 3)

            prep = [0]

            def prepared(ins, wait=False):
                prep[0] += 1
                ins.then_inc(s_prep, 1)
                if wait:
                    dve.wait_ge(s_prep, prep[0])

            def split(hi, lo, raw, arrived, count):
                dve.wait_ge(arrived, count)
                prepared(nc.vector.tensor_copy(hi, raw), wait=True)
                prepared(nc.vector.tensor_tensor(lo, raw, hi.bitcast(f32), ALU.subtract))

            dve.wait_ge(s_halo, 16 * 4)
            for _ in statistics(0, lambda j: XH[:, j, :], HALO):
                pass
            for _ in group_statistics(0):
                pass
            split(wp_hi[:], wp_lo[:], wp_raw, s_wp, 16)
            dve.wait_ge(s_bias, 16 * 4)
            dve.wait_ge(s_zero, 2)
            prepared(nc.vector.tensor_copy(ones_r[:], const_raw[:, C_ONES - C_KEEP:C_ONES - C_KEEP + P]))
            proj = slice(0, B_PROJ)
            prepared(nc.vector.tensor_copy(bias_hi[:, proj], bias_raw[:, proj]), wait=True)
            prepared(nc.vector.tensor_copy(bias_r[0:1, proj], bias_hi[0:1, proj].bitcast(f32)))
            prepared(nc.vector.tensor_tensor(bias_r[32:33, proj], bias_raw[32:33, proj],
                                             bias_hi[32:33, proj].bitcast(f32), ALU.subtract))
            assert prep[0] == PREP_PROJ
            low_part(0, (HALF, HALO - HALF))
            prepared(nc.vector.tensor_copy(bv_rep, spread(bv_col, [0, 64])))
            assert prep[0] == PREP_BV
            body(-2)
            split(w1_hi[:], w1_lo[:], w1_raw, s_w1, 16)
            prepared(nc.vector.tensor_copy(sel_r[:], const_raw[:, 0:CHUNKS * P]))
            dve.wait_ge(s_bvo, 1)
            full = slice(B_PROJ, B_ALL)
            prepared(nc.vector.tensor_tensor(bias_raw[:, full], gbank[1][0:64, 0:DIM], bias_raw[:, full],
                                             ALU.add), wait=True)
            prepared(nc.vector.tensor_copy(bias_hi[:, full], bias_raw[:, full]), wait=True)
            prepared(nc.vector.tensor_copy(bias_r[0:1, full], bias_hi[0:1, full].bitcast(f32)))
            prepared(nc.vector.tensor_tensor(bias_r[32:33, full], bias_raw[32:33, full],
                                             bias_hi[32:33, full].bitcast(f32), ALU.subtract))
            assert prep[0] == PREP_ALL
            for t in (-1, 0):
                body(t)
            with dve.Fori(1, GROUPS - 3) as t:
                body(t)
            for t in (GROUPS - 3, GROUPS - 2, GROUPS - 1):
                body(t)
            for h in range(2):
                result(GROUPS - 1, h)

        @block.tensor
        def _(pe):
            def transposes(stage, counts):
                pe.wait_ge(s_xn, stage + 1)
                for h, count in enumerate(counts):
                    if isinstance(stage, int) and stage == 1:
                        pe.wait_ge(s_qkv_sb, HALF + h)
                    elif past(stage, 2):
                        pe.wait_ge(s_hid, 2 * CHUNKS * (stage - 1) - 1 + h)
                    for j in range(count):
                        last = nc.tensor.transpose(front[h][:, j * P:(j + 1) * P],
                                                   xn[:, h * HALF + j, :], ident)
                    last.then_inc(s_xT, 1)

            def project(n, positions, width):
                for j in positions:
                    if j == 0:
                        pe.wait_ge(s_xlo, 2 * (n + 1) + 2)
                    if j >= 3:
                        pe.wait_ge(s_qkv_sb, projected(n, j - 3) if past(n, 0) else j - 2)
                    elif j == 2 and isinstance(n, int) and n == 0:
                        pe.wait_ge(s_qkv_sb, HALO)
                    elif j == 2 and past(n, 1):
                        pe.wait_ge(s_hid, 2 * CHUNKS * n - 2)
                    bank = rounds[j % 3]
                    nc.tensor.matmul(bank[:, DIM:width], ones_r[:], bias_r[:, 0:width - DIM],
                                     start=True, stop=False, skip_group_check=True)
                    for a, b in ((x_hi, wp_lo), (x_lo, wp_hi), (x_hi, wp_hi)):
                        last = nc.tensor.matmul(bank[:, 0:width], a[:, j, :], b[:, 0:width], start=False,
                                                stop=a is x_hi and b is wp_hi, skip_group_check=True)
                    last.then_inc(s_qkv, 1)

            def scores_T(t):
                pe.wait_ge(s_qk, 2 * t + 1)
                if past(t, 1):
                    pe.wait_ge(s_oT_sb, 2 * t - 1)
                for j in range(HALF):
                    for d in range(HEAD_DIM):
                        p = bass.AP(prod[0][:].tensor, j * WINDOW * DIM + d,
                                    [list(prod[0][:].ap[0]), [HEAD_DIM, WH]])
                        last = nc.tensor.matmul(chain[0][0:WH, j * P:(j + 1) * P], p, ident,
                                                is_transpose=True, start=d == 0, stop=d == HEAD_DIM - 1)
                last.then_inc(s_scT, 1)

            def scores(t):
                pe.wait_ge(s_scT_sb, t + 1)
                for j in range(HALF):
                    last = nc.tensor.transpose(chain[0][:, j * WH:(j + 1) * WH],
                                               scT[0:WH, j * P:(j + 1) * P], ident[0:WH, 0:WH])
                last.then_inc(s_score[0], 1)

            def experts_out(t, h):
                pe.wait_ge(s_hidg, 2 * CHUNKS * t + (h + 1) * CHUNKS)
                if past(t, 1):
                    pe.wait_ge(s_res, 2 * t + h - 1)
                nc.tensor.matmul(ybank[h][:], ones_r[:], spread(bias_r[:, B_PROJ:B_PROJ + 1], [0, HALF], [1, DIM]),
                                 start=True, stop=False, skip_group_check=True)
                for j in range(HALF):
                    for m in range(CHUNKS):
                        last = nc.tensor.matmul(ybank[h][:, j * DIM:(j + 1) * DIM],
                                                hidg[:, h * CHUNKS + m, j * P:(j + 1) * P],
                                                w2_sb[:, m, :],
                                                start=False, stop=False, skip_group_check=True)
                last.then_inc(s_w2, 1)

            def hidden(n, chunks):
                for i in chunks:
                    if i < 2:
                        pe.wait_ge(s_qkv_sb, projected(n, GROUP - 2 + i))
                    elif i == 2:
                        pe.wait_ge(s_qkv_sb, projected(n, GROUP - 3))
                        if past(n, 1):
                            pe.wait_ge(s_dif, 2 * n)
                    else:
                        pe.wait_ge(s_hid, 2 * CHUNKS * n + i - 2)
                    h, m = i // CHUNKS, i % CHUNKS
                    for a, b in ((w1_lo, x_hi), (w1_hi, x_lo), (w1_hi, x_hi)):
                        last = nc.tensor.matmul(rounds[i % 3][:], a[:, m * P:(m + 1) * P],
                                                b[:, h * HALF:(h + 1) * HALF, :],
                                                start=a is w1_lo, stop=a is w1_hi and b is x_hi)
                    last.then_inc(s_h, 1)

            def gates_T(n):
                pe.wait_ge(s_gate, n + 1)
                if past(n, 1):
                    pe.wait_ge(s_hidg, 2 * CHUNKS * n)
                for h in range(2):
                    for j in range(HALF):
                        last = nc.tensor.transpose(gbank[h][0:2 * EXPERTS, j * P:(j + 1) * P],
                                                   gates[:, h * HALF + j, :].bitcast(f32), ident)
                    last.then_inc(s_gT, 1)

            def gates_spread(n, pair):
                for i in (2 * pair, 2 * pair + 1):
                    h, m = i // CHUNKS, i % CHUNKS
                    if i < 2:
                        pe.wait_ge(s_gT_sb, 2 * n + 2)
                    else:
                        pe.wait_ge(s_hidg, 2 * CHUNKS * n + i - 1)
                    nc.tensor.matmul(gbank[i % 2][:], sel_r[:, m * P:(m + 1) * P],
                                     gT[:, h * HD:(h + 1) * HD], start=True, stop=True)\
                        .then_inc(s_gb, 1)

            def attention_out(t, h):
                pe.wait_ge(s_pv, 2 * t + h + 1)
                if h == 1:
                    if active(t + 2):
                        pe.wait_ge(s_qkv_sb, projected(t + 2, GROUP - 3))
                    elif active(t + 1):
                        pe.wait_ge(s_hid, 2 * CHUNKS * (t + 2) - 2)
                for j in range(HALF):
                    for k in range(WINDOW):
                        last = nc.tensor.matmul(chain[h][:, j * P:(j + 1) * P],
                                                prod[h][:, k, j * DIM:(j + 1) * DIM], ident,
                                                is_transpose=True, start=k == 0, stop=k == WINDOW - 1)
                last.then_inc(s_oT, 1)

            def project_out(t, h):
                pe.wait_ge(s_oT_sb, 2 * t + h + 1)
                for j in range(HALF):
                    last = nc.tensor.matmul(ybank[h][:, j * DIM:(j + 1) * DIM],
                                            oT_sb[h][:, j * P:(j + 1) * P], w_out[:],
                                            start=False, stop=True, skip_group_check=True)
                last.then_inc(s_y, 1)

            def body(t):
                u, v = t + 1, t + 2
                if active(t):
                    if past(t, 1):
                        attention_out(t - 1, 1)
                    scores_T(t)
                    if past(t, 1):
                        project_out(t - 1, 1)
                if active(u):
                    hidden(u, (0, 1))
                if active(t):
                    scores(t)
                    experts_out(t, 0)
                if active(u):
                    gates_T(u)
                if active(t):
                    experts_out(t, 1)
                if active(u):
                    gates_spread(u, 0)
                    hidden(u, (2, 3, 4))
                    gates_spread(u, 1)
                    hidden(u, (5, 6, 7))
                    gates_spread(u, 2)
                if active(v):
                    transposes(v + 1, (HALF, HALF))
                if active(t):
                    attention_out(t, 0)
                if active(u):
                    gates_spread(u, 3)
                if active(v):
                    project(v, range(4), W_ALL)
                if active(t):
                    project_out(t, 0)
                if active(v):
                    project(v, range(4, GROUP), W_ALL)

            pe.wait_ge(s_const, 16)
            transposes(0, (HALF, HALO - HALF))
            pe.wait_ge(s_prep, PREP_PROJ)
            project(-1, range(HALO), 2 * DIM)
            body(-2)
            pe.wait_ge(s_prep, PREP_BV)
            pe.wait_ge(s_w2in, 16 * 2)
            nc.tensor.matmul(gbank[1][0:64, 0:DIM], bv_rep, w_out[:], start=True, stop=True)\
                .then_inc(s_bvo, 1)
            pe.wait_ge(s_prep, PREP_ALL)
            for t in (-1, 0):
                body(t)
            with pe.Fori(1, GROUPS - 3) as t:
                body(t)
            for t in (GROUPS - 3, GROUPS - 2, GROUPS - 1):
                body(t)
            attention_out(GROUPS - 1, 1)
            project_out(GROUPS - 1, 1)


PREP_PROJ, PREP_BV, PREP_ALL = 6, 7, 14


def kernel(**inputs):
    import numpy as _np
    import concourse.bacc as _bacc
    from concourse import mybir as _mybir
    from concourse.bass_utils import run_bass_kernel_spmd as _run

    nc = _bacc.Bacc("TRN2", target_bir_lowering=False, num_devices=1)
    a = {k: _np.asarray(v) for k, v in inputs.items()}
    b_proj = _np.zeros((64, B_PROJ), _np.float32)
    b_proj[0::32] = _np.concatenate([a["L0_attn_b_k"], a["L0_attn_b_q"], a["L0_ffn_bg"]])
    arrays = {
        "x": a["L0_attn_hidden_states"],
        "w_proj": _np.concatenate([a["L0_attn_w_v"], a["L0_attn_w_k"], a["L0_attn_w_q"],
                                   a["L0_ffn_Wg"].T], axis=1),
        "b_proj": b_proj,
        "b_v": a["L0_attn_b_v"],
        "w_o": a["L0_attn_w_o"],
        "b_o": a["L0_attn_b_o"],
        "w1": a["L0_ffn_W1"].reshape(EXPERTS * RANK, DIM).T,
        "w2": a["L0_ffn_W2"].transpose(0, 2, 1).reshape(EXPERTS * RANK, DIM),
        "const": constants(),
    }
    arrays = {f"in_{k}_dram": _np.ascontiguousarray(v) for k, v in arrays.items()}
    args = [nc.dram_tensor(k, v.shape, _mybir.dt.from_np(v.dtype), kind="ExternalInput").ap()
            for k, v in arrays.items()]
    args.append(nc.dram_tensor("out_0_dram", (BATCH, SEQ, DIM), _mybir.dt.float32, kind="ExternalOutput").ap())
    attention_and_experts(nc, *args)
    r = _run(nc, [arrays], core_ids=[0])
    return r.results[0]["out_0_dram"]
```

```python
import numpy as np
import concourse.bass as bass
from concourse import mybir
from contextlib import ExitStack

BATCH, SEQ, DIM = 16, 512, 128
HEADS, HEAD_DIM = 16, 8
WINDOW, REACH = 7, 3
EXPERTS, RANK = 8, 64
SCALING = 128.0 / RANK
SCALE = HEAD_DIM ** -0.5
EPS = 1e-5
P = 128

TOKENS = BATCH * SEQ
PER = TOKENS // P
PARTS = SEQ // PER
HALO = 2 * REACH
SLOTS = PER + HALO
GROUP = 8
GROUPS = PER // GROUP
HALF = GROUP // 2
V0 = 3 * GROUP
K0 = V0 + 3 * GROUP + REACH
PLACES = K0 + SLOTS
HALO_HALVES = ((0, HALF), (HALF, HALO))
HD = HALF * DIM
WH = WINDOW * HEADS
HW = HALF * HEADS
CHUNKS = EXPERTS * RANK // P
PER_CHUNK = P // RANK
GW = GROUP * EXPERTS

C_IDENT = 0
C_TIE = C_IDENT + P
C_EDGE = C_TIE + GW
C_NORM = C_EDGE + 2
NORM_CONSTANTS = (DIM / 4, 1 / DIM, EPS, -0.5, -1.0)
C_KEEP = C_NORM + GROUP * len(NORM_CONSTANTS)
C_SEL = C_KEEP
C_ONES = C_SEL + CHUNKS * P
C_ALL = C_ONES + P
NEVER = -1e30
TAKEN = -3e38

W_ALL = 3 * DIM + EXPERTS
B_PROJ = W_ALL - DIM
B_ALL = B_PROJ + DIM

NORM_STEPS = 10
TOP_STEPS = 12
GATE_STEPS = 7


def constants():
    c = np.zeros((P, C_ALL), np.float32)
    c[:, C_IDENT:C_IDENT + P] = np.eye(P)
    c[:, C_TIE:C_TIE + GW] = np.tile(np.arange(EXPERTS, 0, -1), GROUP)
    for m in range(CHUNKS):
        for r in range(P):
            for part in range(2):
                c[EXPERTS * part + m * PER_CHUNK + r // RANK, C_SEL + m * P + r] = SCALING
    c[0, C_ONES:C_ONES + P] = 1.0
    c[32, C_ONES:C_ONES + P] = 1.0
    c[0::PARTS, C_EDGE] = NEVER
    c[PARTS - 1::PARTS, C_EDGE + 1] = NEVER
    for i, value in enumerate(NORM_CONSTANTS):
        c[:, C_NORM + i * GROUP:C_NORM + (i + 1) * GROUP] = value
    return c


def past(n, least):
    return not isinstance(n, int) or n >= least


def active(n):
    return not isinstance(n, int) or 0 <= n < GROUPS


def projected(n, j):
    return n * GROUP + j + 1


def attention_and_experts(nc, x, w_proj, b_proj, bv, wo, bo, w1, w2, const, out):
    f32, f32r = mybir.dt.float32, mybir.dt.float32r
    ALU, ACT, AX = mybir.AluOpType, mybir.ActivationFunctionType, mybir.AxisListType.X
    x_tok = x.rearrange("b s h -> (b s) h")
    x_view = x_tok.rearrange("(p j) h -> p j h", j=PER)
    out_view = out.rearrange("b s h -> (b s) h").rearrange("(p j) h -> p j h", j=PER)

    with ExitStack() as ctx:
        def sb(name, shape, dt=f32):
            return ctx.enter_context(nc.sbuf_tensor(name, shape, dt))

        def pb(name):
            return ctx.enter_context(nc.psum_tensor(name, [P, 512], f32))

        def sem(name):
            return ctx.enter_context(nc.semaphore(name))

        X = sb("X", [P, PER, DIM])
        KV = sb("KV", [P, PLACES, DIM])
        KV_end = sb("KV_end", [P, 2, REACH, DIM])
        const_sb = sb("const_sb", [P, C_KEEP])
        wp_hi, wp_lo = (sb(f"wp_{x}", [P, W_ALL], f32r) for x in ("hi", "lo"))
        w1_hi, w1_lo = (sb(f"w1_{x}", [P, CHUNKS * P], f32r) for x in ("hi", "lo"))
        w_out = sb("w_out", [P, DIM])
        w2_sb = sb("w2_sb", [P, CHUNKS, DIM])
        bias_r = sb("bias_r", [64, B_ALL], f32r)
        ones_r = sb("ones_r", [64, P], f32r)
        sel_r = sb("sel_r", [64, CHUNKS * P], f32r)
        def row_buffers(name, count):
            return (sb(f"{name}_st6", [P, count, 6]), sb(f"{name}_mean", [P, count]),
                    sb(f"{name}_dif", [P, count]), sb(f"{name}_rstd", [P, count]),
                    sb(f"{name}_shift", [P, count]))

        group_rows = row_buffers("group", GROUP)
        halo_rows = row_buffers("halo", HALO)
        xn = sb("xn", [P, GROUP, DIM])
        x_hi = sb("x_hi", [P, GROUP, P], f32r)
        x_lo = sb("x_lo", [P, GROUP, P], f32r)
        halo_hi = sb("halo_hi", [P, HALO, P], f32r)
        halo_lo = sb("halo_lo", [P, HALO, P], f32r)
        prod = [sb(f"prod{h}", [P, WINDOW, HD]) for h in range(2)]
        sc = [sb(f"sc{h}", [P, WINDOW, HW]) for h in range(2)]
        smax = [sb(f"smax{h}", [P, HW]) for h in range(2)]
        srec = [sb(f"srec{h}", [P, HW]) for h in range(2)]
        ssum = [sb(f"ssum{h}", [P, HW]) for h in range(2)]
        scT = sb("scT", [P, HD])
        oT_sb = [sb(f"oT_sb{h}", [P, HD]) for h in range(2)]
        y_sb = oT_sb
        hid = sb("hid", [P, 2 * CHUNKS, HD])
        hidg = sb("hidg", [P, 2 * CHUNKS, HD])
        logit = sb("logit", [P, GROUP, EXPERTS])
        g_top = sb("g_top", [P, 4, GROUP])
        g_dif = sb("g_dif", [P, GW])
        g_tmp = sb("g_tmp", [P, GW])
        g_sel1 = sb("g_sel1", [P, GW])
        g_sel2 = sb("g_sel2", [P, GW])
        g_exp = sb("g_exp", [P, GW])
        g_sum = sb("g_sum", [P, GROUP])
        g_w = sb("g_w", [P, GW])
        g_tree = sb("g_tree", [P, GROUP, EXPERTS // 2])
        gates = sb("gates", [P, GROUP, 2 * EXPERTS], f32r)
        gT = sb("gT", [64, GROUP * P], f32r)

        early_at = [0, 0]

        def early(h, rows, *shape):
            steps, size = [], 1
            for n in reversed(shape):
                steps.insert(0, [size, n])
                size *= n
            a = bass.AP(prod[h][:].tensor, early_at[h], [[prod[h][:].ap[0][0], rows], *steps])
            early_at[h] += size
            assert early_at[h] <= WINDOW * HD
            return a

        XH = early(0, P, HALO, DIM)
        wp_raw = early(0, P, W_ALL)
        w1_raw = early(0, P, CHUNKS * P)
        const_raw = early(0, 64, C_ALL - C_KEEP)
        bias_raw = early(0, 64, B_ALL)
        bias_hi = early(0, 64, B_ALL).bitcast(f32r)
        bv_col = early(0, P, 1)
        bv_rep = early(0, P, 64)
        halo_xn = early(1, P, HALO, DIM)

        front = [pb("front0"), pb("front1")]
        gbank = [pb("gbank0"), pb("gbank1")]
        chain = [pb("chain0"), pb("chain1")]
        rounds = [front[0], front[1], chain[1]]
        ybank = [pb("ybank0"), pb("ybank1")]
        halo_T = [ybank[0], ybank[1]]
        halo_banks = [gbank[0], chain[0], ybank[0], ybank[1]]

        ident = const_sb[:, C_IDENT:C_IDENT + P]
        tie = const_sb[:, C_TIE:C_TIE + GW]
        edge = [const_sb[:, C_EDGE:C_EDGE + 1], const_sb[:, C_EDGE + 1:C_EDGE + 2]]
        quarter_dim, per_dim, eps, minus_half, minus_one = (
            const_sb[:, C_NORM + i * GROUP:C_NORM + (i + 1) * GROUP] for i in range(len(NORM_CONSTANTS)))

        s_const = sem("s_const")
        s_bias = sem("s_bias")
        s_wp = sem("s_wp")
        s_w1 = sem("s_w1")
        s_w2in = sem("s_w2in")
        s_halo0 = sem("s_halo0")
        s_halo = sem("s_halo")
        s_halo_stat = sem("s_halo_stat")
        s_halo_rstd = sem("s_halo_rstd")
        s_halo_norm = sem("s_halo_norm")
        s_halo_xn = sem("s_halo_xn")
        s_halo_xT = sem("s_halo_xT")
        s_halo_xhi = sem("s_halo_xhi")
        s_halo_xlo = sem("s_halo_xlo")
        s_halo_kv = sem("s_halo_kv")
        s_halo_kv_sb = sem("s_halo_kv_sb")
        s_x = sem("s_x")
        s_zero = sem("s_zero")
        s_prep = sem("s_prep")
        s_bvo = sem("s_bvo")
        s_stat = sem("s_stat")
        s_rstd = sem("s_rstd")
        s_norm = sem("s_norm")
        s_xn = sem("s_xn")
        s_xT = sem("s_xT")
        s_xraw = sem("s_xraw")
        s_xlo = sem("s_xlo")
        s_qkv = sem("s_qkv")
        s_qkv_sb = sem("s_qkv_sb")
        s_top = sem("s_top")
        s_weigh = sem("s_weigh")
        s_gexp = sem("s_gexp")
        s_gate = sem("s_gate")
        s_gT = sem("s_gT")
        s_gT_sb = sem("s_gT_sb")
        s_gb = sem("s_gb")
        s_h = sem("s_h")
        s_hid = sem("s_hid")
        s_hidg = sem("s_hidg")
        s_qk = sem("s_qk")
        s_scT = sem("s_scT")
        s_scT_sb = sem("s_scT_sb")
        s_score = [sem("s_score0"), sem("s_score1")]
        s_mask = sem("s_mask")
        s_max = sem("s_max")
        s_dif = sem("s_dif")
        s_exp = sem("s_exp")
        s_sum = sem("s_sum")
        s_rec = sem("s_rec")
        s_prob = sem("s_prob")
        s_pv = sem("s_pv")
        s_pv_part = sem("s_pv_part")
        s_oT = sem("s_oT")
        s_oT_sb = sem("s_oT_sb")
        s_w2 = sem("s_w2")
        s_y = sem("s_y")
        s_y_sb = sem("s_y_sb")
        s_res = sem("s_res")
        s_store = sem("s_store")

        def windows(place, first):
            a = KV[:, bass.ds(first + place, HALF), :]
            return bass.AP(a.tensor, a.offset, [list(a.ap[0]), [DIM, WINDOW], [1, HD]])

        def spread(a, *dims):
            return bass.AP(a.tensor, a.offset, [list(a.ap[0]), *map(list, dims)])


        block = ctx.enter_context(nc.Block())

        @block.sync
        def _(sp):
            sp.dma_start(X[:, 0:GROUP, :], x_view[:, 0:GROUP, :]).then_inc(s_x, 16)
            sp.wait_ge(s_halo0, 1)
            for a, b in ((1, 16), (16, P)):
                src = x_tok[a * PER - REACH:b * PER - REACH, :].rearrange("(p j) h -> p j h", j=PER)
                sp.dma_start(XH[a:b, 0:REACH, :], src[:, 0:REACH, :]).then_inc(s_halo, 16)
            for a, b in ((0, P - 16), (P - 16, P - 1)):
                src = x_tok[(a + 1) * PER:(b + 1) * PER, :].rearrange("(p j) h -> p j h", j=PER)
                sp.dma_start(XH[a:b, REACH:HALO, :], src[:, 0:REACH, :]).then_inc(s_halo, 16)
            with sp.Fori(1, GROUPS) as n:
                sp.wait_ge(s_x, 16 * n)
                sp.dma_start(X[:, bass.ds(n * GROUP, GROUP), :],
                             x_view[:, bass.ds(n * GROUP, GROUP), :]).then_inc(s_x, 16)
            with sp.Fori(0, GROUPS - 1) as n:
                sp.wait_ge(s_res, 2 * n + 2)
                sp.dma_start(out_view[:, bass.ds(n * GROUP, GROUP), :],
                             X[:, bass.ds(n * GROUP, GROUP), :]).then_inc(s_store, 16)
            for h in range(2):
                rows = slice(PER - (2 - h) * HALF, PER - (1 - h) * HALF)
                sp.wait_ge(s_res, 2 * (GROUPS - 1) + h + 1)
                sp.dma_start(out_view[:, rows, :], X[:, rows, :]).then_inc(s_store, 16)
            sp.wait_ge(s_store, 16 * (GROUPS + 1))

        @block.gpsimd
        def _(pool):
            nc.gpsimd.memset(XH, 0.0).then_inc(s_halo0, 1)
            pool.wait_ge(s_const, 16)

            def scale_and_shift(rows, count, done, before, arrived, norm, used=None):
                st6, n_mean, dif, rstd, shift = rows
                step = [0]

                def op(out, in0, in1, alu):
                    step[0] += 1
                    nc.gpsimd.tensor_tensor(out, in0, in1, alu).then_inc(done, 1)

                def wait():
                    pool.wait_ge(done, before + step[0])

                def const_of(a):
                    return a[:, 0:count]

                pool.wait_ge(*arrived)
                op(n_mean[:], st6[:, :, 1], st6[:, :, 4], ALU.add)
                op(dif[:], st6[:, :, 1], st6[:, :, 4], ALU.subtract)
                if used:
                    pool.wait_ge(*used)
                op(rstd[:], st6[:, :, 2], st6[:, :, 5], ALU.add)
                wait()
                op(dif[:], dif[:], dif[:], ALU.mult)
                wait()
                op(dif[:], dif[:], const_of(quarter_dim), ALU.mult)
                wait()
                op(rstd[:], rstd[:], dif[:], ALU.add)
                wait()
                op(rstd[:], rstd[:], const_of(per_dim), ALU.mult)
                op(n_mean[:], n_mean[:], const_of(minus_half), ALU.mult)
                wait()
                op(rstd[:], rstd[:], const_of(eps), ALU.add)
                wait()
                op(rstd[:], rstd[:], const_of(minus_half), ALU.pow)
                wait()
                nc.gpsimd.tensor_tensor(shift[:], n_mean[:], rstd[:], ALU.mult).then_inc(norm, 1)
                assert step[0] == NORM_STEPS

            def scale_group(n):
                scale_and_shift(group_rows, GROUP, s_rstd, NORM_STEPS * n, (s_stat, n + 1), s_norm,
                                used=(s_xn, n) if past(n, 1) else None)

            def result(t, h):
                pool.wait_ge(s_y_sb, 2 * t + h + 1)
                xs = X[:, bass.ds(t * GROUP + h * HALF, HALF), :]
                nc.gpsimd.tensor_tensor(xs, xs, y_sb[h][:].rearrange("p (j n) -> p j n", j=HALF),
                                        ALU.add).then_inc(s_res, 1)

            def low_part(n):
                for h in range(2):
                    pool.wait_ge(s_xraw, 2 * n + h + 1)
                    rows = slice(h * HALF, (h + 1) * HALF)
                    nc.gpsimd.tensor_tensor(x_lo[:, rows, :], xn[:, rows, :], x_hi[:, rows, :].bitcast(f32),
                                            ALU.subtract).then_inc(s_xlo, 1)

            def weigh(n):
                step = [0]

                def op(out, in0, in1, alu):
                    step[0] += 1
                    nc.gpsimd.tensor_tensor(out, in0, in1, alu).then_inc(s_weigh, 1)
                    pool.wait_ge(s_weigh, GATE_STEPS * n + step[0])

                def by_token(a):
                    return spread(a, [EXPERTS, GROUP], [1, EXPERTS])

                four, weight = g_tree[:], by_token(g_w[:])
                pool.wait_ge(s_gexp, n + 1)
                pool.wait_ge(s_top, TOP_STEPS * (n + 1))
                op(g_w[:], g_exp[:], g_sel1[:], ALU.mult)
                op(four, weight[:, :, 0:4], weight[:, :, 4:8], ALU.add)
                op(four[:, :, 0:2], four[:, :, 0:2], four[:, :, 2:4], ALU.add)
                op(g_sum[:], four[:, :, 0], four[:, :, 1], ALU.add)
                op(g_sum[:], g_sum[:], minus_one, ALU.pow)
                if past(n, 1):
                    pool.wait_ge(s_gT, 2 * n)
                per_sum = spread(g_sum[:, 0:1], [1, GROUP], [0, EXPERTS])
                op(gates[:, :, 0:EXPERTS], weight, per_sum, ALU.mult)
                op(weight, weight, per_sum, ALU.mult)
                nc.gpsimd.tensor_tensor(gates[:, :, EXPERTS:2 * EXPERTS], weight,
                                        gates[:, :, 0:EXPERTS].bitcast(f32), ALU.subtract)\
                    .then_inc(s_gate, 1)
                assert step[0] == GATE_STEPS

            def probabilities(t, h):
                pool.wait_ge(s_rec, 2 * t + h + 1)
                nc.gpsimd.tensor_tensor(sc[h][:], sc[h][:],
                                        spread(srec[h][:, 0:1], [0, WINDOW], [1, HW]),
                                        ALU.mult).then_inc(s_prob, 1)

            def body(t):
                if active(t) and past(t, 1):
                    result(t - 1, 0)
                if active(t + 1):
                    weigh(t + 1)
                if active(t) and past(t, 1):
                    result(t - 1, 1)
                if active(t + 3):
                    scale_group(t + 3)
                if active(t):
                    for h in range(2):
                        probabilities(t, h)
                if active(t + 2):
                    low_part(t + 2)

            scale_group(0)
            scale_and_shift(halo_rows, HALO, s_halo_rstd, 0, (s_halo_stat, 1), s_halo_norm)
            scale_group(1)
            scale_group(2)
            weigh(0)
            body(0)
            with pool.Fori(1, GROUPS - 3) as t:
                body(t)
            for t in (GROUPS - 3, GROUPS - 2, GROUPS - 1):
                body(t)

        @block.scalar
        def _(act):
            act.dma_start(const_sb[:], const[:, 0:C_KEEP]).then_inc(s_const, 16)
            act.dma_start(wp_raw, w_proj).then_inc(s_wp, 16)
            act.dma_start(bias_raw[:, 0:B_PROJ], b_proj).then_inc(s_bias, 16)
            act.dma_start(bias_raw[:, B_PROJ:], bo.rearrange("(a n) -> a n", a=1).broadcast_to([64, DIM]))\
                .then_inc(s_bias, 16)
            act.dma_start(const_raw, const[0:64, C_KEEP:C_ALL]).then_inc(s_bias, 16)
            act.dma_start(bv_col, bv.rearrange("(p a) -> p a", a=1)).then_inc(s_bias, 16)
            act.dma_start(w1_raw, w1).then_inc(s_w1, 16)
            act.dma_start(w_out[:], wo).then_inc(s_w2in, 16)
            act.dma_start(w2_sb[:], w2.rearrange("(c p) n -> p c n", p=P)).then_inc(s_w2in, 16)

            def normalise(n):
                rstd, shift = group_rows[3:]
                act.wait_ge(s_norm, n + 1)
                act.wait_ge(s_xlo, 2 * n)
                for j in range(GROUP):
                    last = act.activation(xn[:, j, :], X[:, bass.ds(n * GROUP + j, 1), :], ACT.Identity,
                                          bias=shift[:, j:j + 1], scale=rstd[:, j:j + 1])
                last.then_inc(s_xn, 1)

            def normalise_halo():
                rstd, shift = halo_rows[3:]
                act.wait_ge(s_halo_norm, 1)
                for j in range(HALO):
                    last = act.activation(halo_xn[:, j, :], XH[:, j, :], ACT.Identity,
                                          bias=shift[:, j:j + 1], scale=rstd[:, j:j + 1])
                last.then_inc(s_halo_xn, 1)

            def transposed_in(n, whole=True):
                for h in range(2):
                    act.wait_ge(s_xT, 2 * n + h + 1)
                    rows = slice(h * HALF, (h + 1) * HALF)
                    last = act.activation(x_hi[:, rows, :], front[h][:], ACT.Copy)
                    if whole:
                        last = act.activation(xn[:, rows, :], front[h][:], ACT.Copy)
                    last.then_inc(s_xraw, 1)

            def halo_high_part():
                for h, (a, b) in enumerate(HALO_HALVES):
                    act.wait_ge(s_halo_xT, h + 1)
                    act.activation(halo_hi[:, a:b, :], halo_T[h][:, 0:(b - a) * P], ACT.Copy)\
                        .then_inc(s_halo_xhi, 1)

            def halo_in():
                for j in range(HALO):
                    act.wait_ge(s_halo_kv, j + 1)
                    if j < REACH:
                        dst = spread(KV[:, V0 + j, 0:1], [(K0 - V0) * DIM, 2], [1, DIM])
                    else:
                        dst = KV_end[:, :, j - REACH, :]
                    bank = halo_banks[j % len(halo_banks)]
                    act.activation(dst, bank[:, 0:2 * DIM].rearrange("p (c n) -> p c n", c=2),
                                   ACT.Copy).then_inc(s_halo_kv_sb, 1)

            def group_in(n):
                for j in range(GROUP):
                    act.wait_ge(s_qkv, projected(n, j))
                    if j == 0 and past(n, 3):
                        act.wait_ge(s_pv, 2 * n - 4)
                        act.wait_ge(s_qk, 2 * n - 4)
                    v = KV[:, bass.ds(n * GROUP + (V0 + REACH + j), 1), :]
                    act.activation(spread(v, [(K0 - V0) * DIM, 2], [1, DIM]),
                                   rounds[j % 3][:, 0:2 * DIM].rearrange("p (c n) -> p c n", c=2), ACT.Copy)
                    act.activation(KV[:, bass.ds(n * GROUP + j, 1), :],
                                   rounds[j % 3][:, 2 * DIM:3 * DIM], ACT.Copy)
                    if j == 0 and past(n, 1):
                        act.wait_ge(s_top, TOP_STEPS * (n - 1) + 2)
                    act.activation(logit[:, j, :], rounds[j % 3][:, 3 * DIM:W_ALL], ACT.Copy)\
                        .then_inc(s_qkv_sb, 1)

            def hidden(n, chunks):
                for i in chunks:
                    act.wait_ge(s_h, 2 * CHUNKS * n + i + 1)
                    if past(n, 1):
                        act.wait_ge(s_hidg, 2 * CHUNKS * (n - 1) + i + 1)
                    act.activation(hid[:, i, :], rounds[i % 3][:], ACT.Gelu).then_inc(s_hid, 1)

            def gates_in(n):
                if past(n, 1):
                    act.wait_ge(s_gb, 2 * CHUNKS * n)
                for h in range(2):
                    act.wait_ge(s_gT, 2 * n + h + 1)
                    act.activation(gT[0:2 * EXPERTS, h * HD:(h + 1) * HD],
                                   gbank[h][0:2 * EXPERTS, :], ACT.Copy).then_inc(s_gT_sb, 1)

            def exponentials(t, h):
                act.wait_ge(s_dif, 2 * t + h + 1)
                act.activation(sc[h][:], sc[h][:], ACT.Exp, scale=SCALE).then_inc(s_exp, 1)

            def attention_in(t, h):
                act.wait_ge(s_oT, 2 * t + h + 1)
                if past(t, 1):
                    act.wait_ge(s_res, 2 * t + h - 1)
                act.activation(oT_sb[h][:], chain[h][:], ACT.Copy).then_inc(s_oT_sb, 1)

            def gate_exp(n):
                act.wait_ge(s_top, TOP_STEPS * n + 2)
                if past(n, 1):
                    act.wait_ge(s_gate, n)
                act.activation(g_exp[:], g_dif[:], ACT.Exp).then_inc(s_gexp, 1)

            def scores_in(t):
                act.wait_ge(s_scT, t + 1)
                act.activation(scT[0:WH, :], chain[0][0:WH, :], ACT.Copy).then_inc(s_scT_sb, 1)

            def halo_end_in():
                act.wait_ge(s_qk, 2 * (GROUPS - 2))
                end = spread(KV[:, V0 + REACH + PER, 0:1], [(K0 - V0) * DIM, 2], [1, REACH * DIM])
                act.activation(end, KV_end[:].rearrange("p c j n -> p c (j n)"), ACT.Copy)\
                    .then_inc(s_qkv_sb, 1)

            def output_in(t, h):
                act.wait_ge(s_y, 2 * t + h + 1)
                act.activation(y_sb[h][:], ybank[h][:], ACT.Copy).then_inc(s_y_sb, 1)

            def body(t):
                if active(t + 1):
                    gate_exp(t + 1)
                if active(t) and past(t, 1):
                    attention_in(t - 1, 1)
                if active(t):
                    scores_in(t)
                    if past(t, 1):
                        output_in(t - 1, 1)
                if active(t + 2):
                    normalise(t + 2)
                if active(t + 1):
                    gates_in(t + 1)
                if active(t):
                    for h in range(2):
                        exponentials(t, h)
                if active(t + 1):
                    hidden(t + 1, range(2 * CHUNKS))
                if active(t + 2):
                    transposed_in(t + 2)
                if active(t):
                    attention_in(t, 0)
                if active(t + 2):
                    group_in(t + 2)
                elif t + 2 == GROUPS:
                    halo_end_in()
                if active(t) and active(t + 1):
                    output_in(t, 0)

            transposed_in(0, whole=False)
            normalise_halo()
            group_in(0)
            halo_high_part()
            gate_exp(0)
            hidden(0, (0, 1, 2))
            halo_in()
            hidden(0, range(3, 2 * CHUNKS))
            transposed_in(1, whole=False)
            gates_in(0)
            group_in(1)
            body(0)
            with act.Fori(1, GROUPS - 3) as t:
                body(t)
            for t in (GROUPS - 3, GROUPS - 2, GROUPS - 1):
                body(t)
            attention_in(GROUPS - 1, 1)

        @block.vector
        def _(dve):
            nc.vector.memset(bias_r[:].bitcast(f32), 0.0).then_inc(s_zero, 1)
            nc.vector.memset(gT[:].bitcast(f32), 0.0).then_inc(s_zero, 1)

            def statistics(n):
                dve.wait_ge(s_x, 16 * (n + 1))
                if past(n, 1):
                    dve.wait_ge(s_norm, n)
                for j in range(GROUP):
                    last = nc.vector.bn_stats(group_rows[0][:, j, :], X[:, bass.ds(n * GROUP + j, 1), :])
                    if j == GROUP - 1:
                        last.then_inc(s_stat, 1)
                    yield

            def early_normalise(n):
                rstd, shift = group_rows[3:]
                dve.wait_ge(s_norm, n + 1)
                if n > 0:
                    dve.wait_ge(s_xT, 2 * n)
                for j in range(GROUP):
                    last = nc.vector.tensor_scalar(xn[:, j, :], X[:, n * GROUP + j, :], rstd[:, j:j + 1],
                                                   shift[:, j:j + 1], ALU.mult, ALU.add)
                last.then_inc(s_xn, 1)

            def early_low_part(n):
                for h in range(2):
                    dve.wait_ge(s_xraw, 2 * n + h + 1)
                    rows = slice(h * HALF, (h + 1) * HALF)
                    nc.vector.tensor_tensor(x_lo[:, rows, :], front[h][:].rearrange("p (j n) -> p j n", n=P),
                                            x_hi[:, rows, :].bitcast(f32), ALU.subtract).then_inc(s_xlo, 1)

            def halo_low_part():
                for h, (a, b) in enumerate(HALO_HALVES):
                    dve.wait_ge(s_halo_xhi, h + 1)
                    nc.vector.tensor_tensor(
                        halo_lo[:, a:b, :], halo_T[h][:, 0:(b - a) * P].rearrange("p (j n) -> p j n", n=P),
                        halo_hi[:, a:b, :].bitcast(f32), ALU.subtract).then_inc(s_halo_xlo, 1)
                    yield

            def choose(n, between):
                step = [0]

                def done(ins):
                    step[0] += 1
                    ins.then_inc(s_top, 1)
                    between()
                    dve.wait_ge(s_top, TOP_STEPS * n + step[0])

                def each(i):
                    return spread(g_top[:, i, 0:1], [1, GROUP], [0, EXPERTS])

                def by_token(a):
                    return spread(a, [EXPERTS, GROUP], [1, EXPERTS])

                dve.wait_ge(s_qkv_sb, projected(n, GROUP - 1))
                if past(n, 1):
                    dve.wait_ge(s_gexp, n)
                done(nc.vector.tensor_reduce(g_top[:, 0, :], logit[:], AX, ALU.max))
                done(nc.vector.tensor_tensor(by_token(g_dif[:]), logit[:], each(0), ALU.subtract))
                if past(n, 1):
                    dve.wait_ge(s_gate, n)
                done(nc.vector.scalar_tensor_tensor(g_tmp[:], g_dif[:], 0.0, tie, ALU.is_equal, ALU.mult))
                done(nc.vector.tensor_reduce(g_top[:, 1, :], by_token(g_tmp[:]), AX, ALU.max))
                done(nc.vector.tensor_tensor(by_token(g_sel1[:]), by_token(g_tmp[:]), each(1), ALU.is_equal))
                done(nc.vector.scalar_tensor_tensor(g_sel2[:], g_sel1[:], TAKEN, g_dif[:], ALU.mult, ALU.add))
                done(nc.vector.tensor_reduce(g_top[:, 2, :], by_token(g_sel2[:]), AX, ALU.max))
                done(nc.vector.tensor_tensor(by_token(g_tmp[:]), by_token(g_sel2[:]), each(2), ALU.is_equal))
                done(nc.vector.tensor_tensor(g_tmp[:], g_tmp[:], tie, ALU.mult))
                done(nc.vector.tensor_reduce(g_top[:, 3, :], by_token(g_tmp[:]), AX, ALU.max))
                done(nc.vector.tensor_tensor(by_token(g_sel2[:]), by_token(g_tmp[:]), each(3), ALU.is_equal))
                step[0] += 1
                nc.vector.tensor_tensor(g_sel1[:], g_sel1[:], g_sel2[:], ALU.add).then_inc(s_top, 1)
                assert step[0] == TOP_STEPS

            def products(t, h):
                if isinstance(t, int) and t == 0:
                    dve.wait_ge(s_halo_kv_sb, HALO)
                    if h == 1:
                        dve.wait_ge(s_qkv_sb, projected(1, REACH - 1))
                elif not active(t + 1) and h == 1:
                    dve.wait_ge(s_qkv_sb, projected(t + 1, 0))
                if past(t, 1):
                    dve.wait_ge(s_oT, 2 * t + h - 1)
                slot = t * GROUP + h * HALF
                q = KV[:, bass.ds(slot, HALF), :]
                nc.vector.tensor_tensor(
                    spread(prod[h][:, 0, 0:1], [DIM, WINDOW], [WINDOW * DIM, HALF], [1, DIM]),
                    spread(q, [0, WINDOW], [DIM, HALF], [1, DIM]),
                    spread(windows(K0, slot), [DIM, WINDOW], [DIM, HALF], [1, DIM]),
                    ALU.mult).then_inc(s_qk, 1)

            def scores(t):
                dve.wait_ge(s_qk, 2 * t + 2)
                if past(t, 1):
                    dve.wait_ge(s_oT_sb, 2 * t)
                nc.vector.tensor_reduce(chain[1][:, 0:HALF * WH],
                                        spread(prod[1][:, 0, 0:1], [HEAD_DIM, HALF * WH], [1, HEAD_DIM]),
                                        AX, ALU.add).then_inc(s_score[1], 1)

            def maximum(t, h):
                dve.wait_ge(s_score[h], t + 1)
                s = chain[h][:, 0:HALF * WH]
                masks = []
                if isinstance(t, int) and t == 0 and h == 0:
                    masks = [(j, 0, REACH - j, 0) for j in range(REACH)]
                if not active(t + 1) and h == 1:
                    masks = [(HALF - 1 - i, WINDOW - REACH + i, WINDOW, 1) for i in range(REACH)]
                for i, (j, a, b, side) in enumerate(masks):
                    part = s[:, j * WH + a * HEADS:j * WH + b * HEADS]
                    ins = nc.vector.tensor_scalar(part, part, edge[side], None, ALU.add)
                    if i == len(masks) - 1:
                        ins.then_inc(s_mask, 1)
                        dve.wait_ge(s_mask, side + 1)
                nc.vector.tensor_reduce(
                    spread(smax[h][:, 0:1], [HEADS, HALF], [1, HEADS]),
                    spread(s, [WH, HALF], [1, HEADS], [HEADS, WINDOW]), AX, ALU.max).then_inc(s_max, 1)

            def less_maximum(t, h):
                dve.wait_ge(s_max, 2 * t + h + 1)
                nc.vector.tensor_tensor(
                    spread(sc[h][:, 0, 0:1], [HW, WINDOW], [HEADS, HALF], [1, HEADS]),
                    spread(chain[h][:, 0:1], [HEADS, WINDOW], [WH, HALF], [1, HEADS]),
                    spread(smax[h][:, 0:1], [0, WINDOW], [HEADS, HALF], [1, HEADS]),
                    ALU.subtract).then_inc(s_dif, 1)

            def total(t, h):
                dve.wait_ge(s_exp, 2 * t + h + 1)
                nc.vector.tensor_reduce(ssum[h][:], spread(sc[h][:, 0, 0:1], [1, HW], [HW, WINDOW]),
                                        AX, ALU.add).then_inc(s_sum, 1)

            def inverse(t, h):
                dve.wait_ge(s_sum, 2 * t + h + 1)
                nc.vector.reciprocal(srec[h][:], ssum[h][:]).then_inc(s_rec, 1)

            def weighted(t, h, parts=1):
                dve.wait_ge(s_prob, 2 * t + h + 1)
                count = HALF // parts
                for first in range(0, HALF, count):
                    pairs = count * HEADS
                    last = nc.vector.tensor_tensor(
                        spread(prod[h][:, 0, first * DIM:first * DIM + 1],
                               [HD, WINDOW], [HEAD_DIM, pairs], [1, HEAD_DIM]),
                        spread(sc[h][:, 0, first * HEADS:first * HEADS + 1],
                               [HW, WINDOW], [1, pairs], [0, HEAD_DIM]),
                        spread(windows(V0, t * GROUP + h * HALF + first),
                               [DIM, WINDOW], [HEAD_DIM, pairs], [1, HEAD_DIM]),
                        ALU.mult)
                    if first + count < HALF:
                        last.then_inc(s_pv_part, 1)
                last.then_inc(s_pv, 1)

            def last_result(h):
                t = GROUPS - 1
                dve.wait_ge(s_y, 2 * t + h + 1)
                xs = X[:, t * GROUP + h * HALF:t * GROUP + (h + 1) * HALF, :]
                nc.vector.tensor_tensor(xs, xs, ybank[h][:].rearrange("p (j n) -> p j n", j=HALF),
                                        ALU.add).then_inc(s_res, 1)

            def gate(n, pair):
                for _ in gate_chunks(n, (2 * pair, 2 * pair + 1)):
                    pass

            def gate_chunks(n, chunks):
                for i in chunks:
                    dve.wait_ge(s_hid, 2 * CHUNKS * n + i + 1)
                    dve.wait_ge(s_gb, 2 * CHUNKS * n + i + 1)
                    if i % CHUNKS == 0 and past(n, 1):
                        dve.wait_ge(s_w2, 2 * (n - 1) + i // CHUNKS + 1)
                    nc.vector.tensor_tensor(hidg[:, i, :], hid[:, i, :], gbank[i % 2][:],
                                            ALU.mult).then_inc(s_hidg, 1)
                    yield

            def fillers(t):
                if not past(t, 1):
                    yield from gate_chunks(0, (4, 5))
                if active(t + 3):
                    yield from statistics(t + 3)
                if not past(t, 1):
                    yield from gate_chunks(0, (6, 7))

            def body(t):
                if active(t) and past(t, 1):
                    products(t, 0)
                rest = fillers(t)
                if active(t + 1):
                    choose(t + 1, lambda: next(rest, None))
                for _ in rest:
                    pass
                if active(t) and past(t, 1):
                    products(t, 1)
                if active(t):
                    scores(t)
                    for h in range(2):
                        maximum(t, h)
                    for h in range(2):
                        less_maximum(t, h)
                    for h in range(2):
                        total(t, h)
                    for h in range(2):
                        inverse(t, h)
                if active(t + 1):
                    gate(t + 1, 0)
                if active(t):
                    weighted(t, 0, parts=1 if active(t + 1) else LAST_PARTS)
                if active(t + 1):
                    gate(t + 1, 1)
                    gate(t + 1, 2)
                if active(t):
                    weighted(t, 1, parts=1 if active(t + 1) else LAST_PARTS)
                if active(t + 1):
                    gate(t + 1, 3)

            prep = [0]

            def prepared(ins, wait=False):
                prep[0] += 1
                ins.then_inc(s_prep, 1)
                if wait:
                    dve.wait_ge(s_prep, prep[0])

            def split(hi, lo, raw, arrived, count):
                dve.wait_ge(arrived, count)
                prepared(nc.vector.tensor_copy(hi, raw), wait=True)
                prepared(nc.vector.tensor_tensor(lo, raw, hi.bitcast(f32), ALU.subtract))

            for _ in statistics(0):
                pass
            dve.wait_ge(s_halo, 16 * 4)
            for j in range(HALO):
                last = nc.vector.bn_stats(halo_rows[0][:, j, :], XH[:, j, :])
            last.then_inc(s_halo_stat, 1)
            split(wp_hi[:], wp_lo[:], wp_raw, s_wp, 16)
            dve.wait_ge(s_bias, 16 * 4)
            dve.wait_ge(s_zero, 2)
            prepared(nc.vector.tensor_copy(ones_r[:], const_raw[:, C_ONES - C_KEEP:C_ONES - C_KEEP + P]))
            proj = slice(0, B_PROJ)
            prepared(nc.vector.tensor_copy(bias_hi[:, proj], bias_raw[:, proj]), wait=True)
            prepared(nc.vector.tensor_copy(bias_r[0:1, proj], bias_hi[0:1, proj].bitcast(f32)))
            prepared(nc.vector.tensor_tensor(bias_r[32:33, proj], bias_raw[32:33, proj],
                                             bias_hi[32:33, proj].bitcast(f32), ALU.subtract))
            assert prep[0] == PREP_PROJ
            early_normalise(0)
            for _ in statistics(1):
                pass
            early_low_part(0)
            prepared(nc.vector.tensor_copy(bv_rep, spread(bv_col, [0, 64])))
            assert prep[0] == PREP_BV
            split(w1_hi[:], w1_lo[:], w1_raw, s_w1, 16)
            prepared(nc.vector.tensor_copy(sel_r[:], const_raw[:, 0:CHUNKS * P]))
            assert prep[0] == PREP_W1
            early_normalise(1)
            for _ in statistics(2):
                pass
            halo_low = halo_low_part()
            choose(0, lambda: next(halo_low, None))
            dve.wait_ge(s_bvo, 1)
            full = slice(B_PROJ, B_ALL)
            prepared(nc.vector.tensor_tensor(bias_raw[:, full], gbank[1][0:64, 0:DIM], bias_raw[:, full],
                                             ALU.add), wait=True)
            prepared(nc.vector.tensor_copy(bias_hi[:, full], bias_raw[:, full]), wait=True)
            prepared(nc.vector.tensor_copy(bias_r[0:1, full], bias_hi[0:1, full].bitcast(f32)))
            prepared(nc.vector.tensor_tensor(bias_r[32:33, full], bias_raw[32:33, full],
                                             bias_hi[32:33, full].bitcast(f32), ALU.subtract))
            assert prep[0] == PREP_ALL
            dve.wait_ge(s_prep, PREP_ALL)
            products(0, 0)
            early_low_part(1)
            gate(0, 0)
            gate(0, 1)
            products(0, 1)
            body(0)
            with dve.Fori(1, GROUPS - 3) as t:
                body(t)
            for t in (GROUPS - 3, GROUPS - 2, GROUPS - 1):
                body(t)
            for h in range(2):
                last_result(h)

        @block.tensor
        def _(pe):
            def transposes(n):
                pe.wait_ge(s_xn, n + 1)
                for h in range(2):
                    if past(n, 1):
                        pe.wait_ge(s_hid, 2 * CHUNKS * n - 1 + h)
                    for j in range(HALF):
                        last = nc.tensor.transpose(front[h][:, j * P:(j + 1) * P],
                                                   xn[:, h * HALF + j, :], ident)
                    last.then_inc(s_xT, 1)

            def halo_transposes():
                pe.wait_ge(s_halo_xn, 1)
                for h, (a, b) in enumerate(HALO_HALVES):
                    for j in range(a, b):
                        last = nc.tensor.transpose(halo_T[h][:, (j - a) * P:(j - a + 1) * P],
                                                   halo_xn[:, j, :], ident)
                    last.then_inc(s_halo_xT, 1)

            def project_position(bank, hi, lo, width):
                nc.tensor.matmul(bank[:, DIM:width], ones_r[:], bias_r[:, 0:width - DIM],
                                 start=True, stop=False, skip_group_check=True)
                for i, (a, b) in enumerate(((hi, wp_lo), (lo, wp_hi), (hi, wp_hi))):
                    last = nc.tensor.matmul(bank[:, 0:width], a, b[:, 0:width], start=False,
                                            stop=i == 2, skip_group_check=True)
                return last

            def project(n, positions):
                for j in positions:
                    if j == 0:
                        pe.wait_ge(s_xlo, 2 * n + 2)
                    if j >= 3:
                        pe.wait_ge(s_qkv_sb, projected(n, j - 3))
                    elif j == 2 and past(n, 1):
                        pe.wait_ge(s_hid, 2 * CHUNKS * n - 2)
                    project_position(rounds[j % 3], x_hi[:, j, :], x_lo[:, j, :], W_ALL).then_inc(s_qkv, 1)

            def project_halo():
                pe.wait_ge(s_halo_xlo, 2)
                for j in range(HALO):
                    if j >= len(halo_banks):
                        pe.wait_ge(s_halo_kv_sb, j - len(halo_banks) + 1)
                    project_position(halo_banks[j % len(halo_banks)], halo_hi[:, j, :], halo_lo[:, j, :],
                                     2 * DIM).then_inc(s_halo_kv, 1)

            def scores_T(t):
                pe.wait_ge(s_qk, 2 * t + 1)
                if past(t, 1):
                    pe.wait_ge(s_oT_sb, 2 * t - 1)
                for j in range(HALF):
                    for d in range(HEAD_DIM):
                        p = bass.AP(prod[0][:].tensor, j * WINDOW * DIM + d,
                                    [list(prod[0][:].ap[0]), [HEAD_DIM, WH]])
                        last = nc.tensor.matmul(chain[0][0:WH, j * P:(j + 1) * P], p, ident,
                                                is_transpose=True, start=d == 0, stop=d == HEAD_DIM - 1)
                last.then_inc(s_scT, 1)

            def scores(t):
                pe.wait_ge(s_scT_sb, t + 1)
                for j in range(HALF):
                    last = nc.tensor.transpose(chain[0][:, j * WH:(j + 1) * WH],
                                               scT[0:WH, j * P:(j + 1) * P], ident[0:WH, 0:WH])
                last.then_inc(s_score[0], 1)

            def experts_out(t, h, positions):
                if positions[0] == 0:
                    pe.wait_ge(s_hidg, 2 * CHUNKS * t + (h + 1) * CHUNKS)
                    if past(t, 1):
                        pe.wait_ge(s_y_sb, 2 * t + h - 1)
                    nc.tensor.matmul(ybank[h][:], ones_r[:],
                                     spread(bias_r[:, B_PROJ:B_PROJ + 1], [0, HALF], [1, DIM]),
                                     start=True, stop=False, skip_group_check=True)
                for j in positions:
                    for m in range(CHUNKS):
                        last = nc.tensor.matmul(ybank[h][:, j * DIM:(j + 1) * DIM],
                                                hidg[:, h * CHUNKS + m, j * P:(j + 1) * P],
                                                w2_sb[:, m, :],
                                                start=False, stop=False, skip_group_check=True)
                if positions[-1] == HALF - 1:
                    last.then_inc(s_w2, 1)

            def hidden(n, chunks):
                for i in chunks:
                    if i < 2:
                        pe.wait_ge(s_qkv_sb, projected(n, GROUP - 2 + i))
                    elif i == 2:
                        pe.wait_ge(s_qkv_sb, projected(n, GROUP - 3))
                        if past(n, 1):
                            pe.wait_ge(s_dif, 2 * n)
                    else:
                        pe.wait_ge(s_hid, 2 * CHUNKS * n + i - 2)
                    h, m = i // CHUNKS, i % CHUNKS
                    for a, b in ((w1_lo, x_hi), (w1_hi, x_lo), (w1_hi, x_hi)):
                        last = nc.tensor.matmul(rounds[i % 3][:], a[:, m * P:(m + 1) * P],
                                                b[:, h * HALF:(h + 1) * HALF, :],
                                                start=a is w1_lo, stop=a is w1_hi and b is x_hi)
                    last.then_inc(s_h, 1)

            def gates_T(n):
                pe.wait_ge(s_gate, n + 1)
                if past(n, 1):
                    pe.wait_ge(s_hidg, 2 * CHUNKS * n)
                else:
                    pe.wait_ge(s_halo_kv_sb, HALO)
                    pe.wait_ge(s_prep, PREP_BV_IN)
                for h in range(2):
                    for j in range(HALF):
                        last = nc.tensor.transpose(gbank[h][0:2 * EXPERTS, j * P:(j + 1) * P],
                                                   gates[:, h * HALF + j, :].bitcast(f32), ident)
                    last.then_inc(s_gT, 1)

            def gates_spread(n, pair):
                for i in (2 * pair, 2 * pair + 1):
                    h, m = i // CHUNKS, i % CHUNKS
                    if i < 2:
                        pe.wait_ge(s_gT_sb, 2 * n + 2)
                    else:
                        pe.wait_ge(s_hidg, 2 * CHUNKS * n + i - 1)
                    nc.tensor.matmul(gbank[i % 2][:], sel_r[:, m * P:(m + 1) * P],
                                     gT[:, h * HD:(h + 1) * HD], start=True, stop=True)\
                        .then_inc(s_gb, 1)

            def attention_out(t, h):
                parts = 1 if active(t + 1) else LAST_PARTS
                if h == 1:
                    if active(t + 2):
                        pe.wait_ge(s_qkv_sb, projected(t + 2, GROUP - 3))
                    elif active(t + 1):
                        pe.wait_ge(s_hid, 2 * CHUNKS * (t + 2) - 2)
                for j in range(HALF):
                    part, within = divmod(j, HALF // parts)
                    if within == 0 and part < parts - 1:
                        pe.wait_ge(s_pv_part, h * (parts - 1) + part + 1)
                    elif within == 0:
                        pe.wait_ge(s_pv, 2 * t + h + 1)
                    for k in range(WINDOW):
                        last = nc.tensor.matmul(chain[h][:, j * P:(j + 1) * P],
                                                prod[h][:, k, j * DIM:(j + 1) * DIM], ident,
                                                is_transpose=True, start=k == 0, stop=k == WINDOW - 1)
                last.then_inc(s_oT, 1)

            def project_out(t, h):
                pe.wait_ge(s_oT_sb, 2 * t + h + 1)
                for j in range(HALF):
                    last = nc.tensor.matmul(ybank[h][:, j * DIM:(j + 1) * DIM],
                                            oT_sb[h][:, j * P:(j + 1) * P], w_out[:],
                                            start=False, stop=True, skip_group_check=True)
                last.then_inc(s_y, 1)

            def body(t):
                u, v = t + 1, t + 2
                if active(t):
                    if past(t, 1):
                        attention_out(t - 1, 1)
                        scores_T(t)
                        project_out(t - 1, 1)
                if active(u):
                    hidden(u, (0, 1))
                if active(t):
                    scores(t)
                    experts_out(t, 0, (0, 1, 2))
                if active(u) and past(t, 1):
                    gates_T(u)
                if active(t):
                    experts_out(t, 0, (3,))
                    experts_out(t, 1, (0, 1))
                if not past(t, 1):
                    gates_T(u)
                if active(u):
                    gates_spread(u, 0)
                    hidden(u, (2,))
                if active(t):
                    experts_out(t, 1, (2,))
                if active(u):
                    hidden(u, (3, 4))
                    gates_spread(u, 1)
                    hidden(u, (5, 6, 7))
                if active(t):
                    experts_out(t, 1, (3,))
                if active(v):
                    transposes(v)
                if active(u):
                    gates_spread(u, 2)
                if active(t):
                    attention_out(t, 0)
                if active(u):
                    gates_spread(u, 3)
                if active(v):
                    project(v, range(GROUP))
                if active(t) and active(u):
                    project_out(t, 0)

            pe.wait_ge(s_const, 16)
            for _ in range(WARM_UP):
                nc.tensor.transpose(front[0][:, 0:P], ident, ident)
            transposes(0)
            pe.wait_ge(s_prep, PREP_PROJ)
            project(0, range(GROUP))
            halo_transposes()
            pe.wait_ge(s_prep, PREP_W1)
            hidden(0, (0, 1, 2))
            pe.wait_ge(s_w2in, 16 * 2)
            nc.tensor.matmul(gbank[1][0:64, 0:DIM], bv_rep, w_out[:], start=True, stop=True)\
                .then_inc(s_bvo, 1)
            project_halo()
            hidden(0, range(3, 2 * CHUNKS))
            transposes(1)
            gates_T(0)
            for pair in range(CHUNKS - 1):
                project(1, (2 * pair, 2 * pair + 1))
                gates_spread(0, pair)
            project(1, (GROUP - 2, GROUP - 1))
            scores_T(0)
            gates_spread(0, CHUNKS - 1)
            pe.wait_ge(s_prep, PREP_ALL)
            body(0)
            with pe.Fori(1, GROUPS - 3) as t:
                body(t)
            for t in (GROUPS - 3, GROUPS - 2, GROUPS - 1):
                body(t)
            attention_out(GROUPS - 1, 1)
            for h in range(2):
                project_out(GROUPS - 1, h)


WARM_UP = 48
LAST_PARTS = 4
PREP_PROJ, PREP_BV, PREP_W1, PREP_BV_IN, PREP_ALL = 6, 7, 10, 11, 14


def kernel(**inputs):
    import numpy as _np
    import concourse.bacc as _bacc
    from concourse import mybir as _mybir
    from concourse.bass_utils import run_bass_kernel_spmd as _run

    nc = _bacc.Bacc("TRN2", target_bir_lowering=False, num_devices=1)
    a = {k: _np.asarray(v) for k, v in inputs.items()}
    b_proj = _np.zeros((64, B_PROJ), _np.float32)
    b_proj[0::32] = _np.concatenate([a["L0_attn_b_k"], a["L0_attn_b_q"], a["L0_ffn_bg"]])
    arrays = {
        "x": a["L0_attn_hidden_states"],
        "w_proj": _np.concatenate([a["L0_attn_w_v"], a["L0_attn_w_k"], a["L0_attn_w_q"],
                                   a["L0_ffn_Wg"].T], axis=1),
        "b_proj": b_proj,
        "b_v": a["L0_attn_b_v"],
        "w_o": a["L0_attn_w_o"],
        "b_o": a["L0_attn_b_o"],
        "w1": a["L0_ffn_W1"].reshape(EXPERTS * RANK, DIM).T,
        "w2": a["L0_ffn_W2"].transpose(0, 2, 1).reshape(EXPERTS * RANK, DIM),
        "const": constants(),
    }
    arrays = {f"in_{k}_dram": _np.ascontiguousarray(v) for k, v in arrays.items()}
    args = [nc.dram_tensor(k, v.shape, _mybir.dt.from_np(v.dtype), kind="ExternalInput").ap()
            for k, v in arrays.items()]
    args.append(nc.dram_tensor("out_0_dram", (BATCH, SEQ, DIM), _mybir.dt.float32, kind="ExternalOutput").ap())
    attention_and_experts(nc, *args)
    r = _run(nc, [arrays], core_ids=[0])
    return r.results[0]["out_0_dram"]
```
